# Optimizing a Trainium2 kernel written in Bass

```python
import numpy as np
import jax
import jax.numpy as jnp

def _softmax(x, axis=-1):
    return jax.nn.softmax(x, axis=axis)

def _gelu(x):
    return jax.nn.gelu(x, approximate=True)

def _silu(x):
    return jax.nn.silu(x)

def _sigmoid(x):
    return jax.nn.sigmoid(x)

def _layernorm(x, axis=-1, eps=1e-05):
    m = jnp.mean(x, axis=axis, keepdims=True)
    v = jnp.var(x, axis=axis, keepdims=True)
    return (x - m) / jnp.sqrt(v + eps)

def _scatter_add(tgt, idx, src, axis=0):
    return tgt.at[idx].add(src)

def _segment_sum(src, seg, n):
    return jax.ops.segment_sum(src, seg, n)
kernel_name = 'mk_xattn_seq_d1_seqx_r4_2ed9c6'

def setup_inputs(seed: int=0):
    np.random.seed(seed)
    _w = jnp.asarray

    def _rec_inputs():
        import jax
        import jax.numpy as jnp
        _rk = jax.random.key(seed)
        x = 7.22e-05 + 1 * jax.random.normal(jax.random.fold_in(_rk, 1), (16, 256, 512), jnp.float32)
        _lenS = 256 - jax.random.randint(jax.random.fold_in(_rk, 7), (16,), 0, max(1, 256 // 4) + 1, jnp.int32)
        _lenS2 = 256 - jax.random.randint(jax.random.fold_in(_rk, 8), (16,), 0, max(1, 256 // 4) + 1, jnp.int32)
        _ctx_2048P = jax.random.normal(jax.random.fold_in(_rk, 11), (16, 16, 512), jnp.float32)
        _ctx_2048c = jax.random.dirichlet(jax.random.fold_in(_rk, 511), 0.3 * jnp.ones((16,), jnp.float32), (16, 256))
        _ctx_2048t = jnp.einsum('bsk,bkd->bsd', _ctx_2048c, _ctx_2048P)
        _ctx_2048t = _ctx_2048t * jax.lax.rsqrt(jnp.mean(jnp.square(_ctx_2048t)) + 1e-12) * 0.953939
        ctx_2048 = 4.13588e-05 + 0.999923 * (_ctx_2048t + 0.3 * jax.random.normal(jax.random.fold_in(_rk, 611), (16, 256, 512), jnp.float32))
        _validS = jnp.arange(256)[None, :] < _lenS[:, None]
        _validS2 = jnp.arange(256)[None, :] < _lenS2[:, None]
        _causal = jnp.tril(jnp.ones((256, 256), dtype=bool))
        mask_Bx1xSxS2_ff0 = jnp.where(jnp.ones((16, 1, 256, 256), dtype=bool), 0.0, -1000000000.0).astype(jnp.float32)
        return (x, ctx_2048, mask_Bx1xSxS2_ff0)
    x, ctx_2048, mask_Bx1xSxS2_ff0 = _rec_inputs()

    def _L0_xattn_setup():
        import jax, jax.numpy as jnp
        import numpy as np
        H = 512
        NH = 32
        KVH = 8
        HD = H // NH
        GROUPS = NH // KVH
        EPS = 1e-06
        B, L, S = (4, 256, 256)

        def _gqa_forward(hidden_state, encoder_hidden_state, encoder_attention_mask, Wq, bq, Wk, bk, Wv, bv, Wo, bo, gamma, beta):
            b, l, _ = hidden_state.shape
            s = encoder_hidden_state.shape[1]
            q = hidden_state @ Wq + bq
            k = encoder_hidden_state @ Wk + bk
            v = encoder_hidden_state @ Wv + bv
            q = q.reshape(b, l, KVH, GROUPS, HD).transpose(0, 2, 3, 1, 4)
            k = k.reshape(b, s, KVH, HD).transpose(0, 2, 1, 3)
            v = v.reshape(b, s, KVH, HD).transpose(0, 2, 1, 3)
            scale = 1.0 / jnp.sqrt(jnp.asarray(HD, q.dtype))
            scores = jnp.einsum('bkgld,bksd->bkgls', q, k) * scale
            scores = scores + encoder_attention_mask[:, :, None, :, :]
            attn = jax.nn.softmax(scores, axis=-1)
            out = jnp.einsum('bkgls,bksd->bkgld', attn, v)
            out = out.transpose(0, 3, 1, 2, 4).reshape(b, l, H)
            out = out @ Wo + bo
            x = out + hidden_state
            mu = jnp.mean(x, axis=-1, keepdims=True)
            var = jnp.var(x, axis=-1, keepdims=True)
            return (x - mu) * jax.lax.rsqrt(var + EPS) * gamma + beta
        key = jax.random.key(seed)
        ks = jax.random.split(key, 12)
        sd = 0.02
        return {'hidden_state': jax.random.normal(ks[0], (B, L, H), jnp.float32), 'encoder_hidden_state': jax.random.normal(ks[1], (B, S, H), jnp.float32), 'encoder_attention_mask': jnp.zeros((B, 1, L, S), jnp.float32), 'Wq': jax.random.normal(ks[2], (H, H), jnp.float32) * sd, 'bq': jnp.zeros((H,), jnp.float32), 'Wk': jax.random.normal(ks[3], (H, KVH * HD), jnp.float32) * sd, 'bk': jnp.zeros((KVH * HD,), jnp.float32), 'Wv': jax.random.normal(ks[4], (H, KVH * HD), jnp.float32) * sd, 'bv': jnp.zeros((KVH * HD,), jnp.float32), 'Wo': jax.random.normal(ks[5], (H, H), jnp.float32) * sd, 'bo': jnp.zeros((H,), jnp.float32), 'gamma': jnp.ones((H,), jnp.float32), 'beta': jnp.zeros((H,), jnp.float32)}
    _L0_xattn_all = _L0_xattn_setup()
    _L0_xattn_in = {k: v for k, v in _L0_xattn_all.items() if k in ('Wq', 'bq', 'Wk', 'bk', 'Wv', 'bv', 'Wo', 'bo', 'gamma', 'beta')}
    del _L0_xattn_all
    return {'x': x, 'ctx_2048': ctx_2048, 'mask_Bx1xSxS2_ff0': mask_Bx1xSxS2_ff0, 'L0_xattn_Wq': _L0_xattn_in['Wq'], 'L0_xattn_bq': _L0_xattn_in['bq'], 'L0_xattn_Wk': _L0_xattn_in['Wk'], 'L0_xattn_bk': _L0_xattn_in['bk'], 'L0_xattn_Wv': _L0_xattn_in['Wv'], 'L0_xattn_bv': _L0_xattn_in['bv'], 'L0_xattn_Wo': _L0_xattn_in['Wo'], 'L0_xattn_bo': _L0_xattn_in['bo'], 'L0_xattn_gamma': _L0_xattn_in['gamma'], 'L0_xattn_beta': _L0_xattn_in['beta']}

def reference(x, ctx_2048, mask_Bx1xSxS2_ff0, L0_xattn_Wq, L0_xattn_bq, L0_xattn_Wk, L0_xattn_bk, L0_xattn_Wv, L0_xattn_bv, L0_xattn_Wo, L0_xattn_bo, L0_xattn_gamma, L0_xattn_beta):
    import jax
    import jax.numpy as jnp

    def _L0_xattn_ref(hidden_state, encoder_hidden_state, encoder_attention_mask, Wq, bq, Wk, bk, Wv, bv, Wo, bo, gamma, beta):
        import jax, jax.numpy as jnp
        import numpy as np
        H = 512
        NH = 32
        KVH = 8
        HD = H // NH
        GROUPS = NH // KVH
        EPS = 1e-06
        B, L, S = (4, 256, 256)

        def _gqa_forward(hidden_state, encoder_hidden_state, encoder_attention_mask, Wq, bq, Wk, bk, Wv, bv, Wo, bo, gamma, beta):
            b, l, _ = hidden_state.shape
            s = encoder_hidden_state.shape[1]
            q = hidden_state @ Wq + bq
            k = encoder_hidden_state @ Wk + bk
            v = encoder_hidden_state @ Wv + bv
            q = q.reshape(b, l, KVH, GROUPS, HD).transpose(0, 2, 3, 1, 4)
            k = k.reshape(b, s, KVH, HD).transpose(0, 2, 1, 3)
            v = v.reshape(b, s, KVH, HD).transpose(0, 2, 1, 3)
            scale = 1.0 / jnp.sqrt(jnp.asarray(HD, q.dtype))
            scores = jnp.einsum('bkgld,bksd->bkgls', q, k) * scale
            scores = scores + encoder_attention_mask[:, :, None, :, :]
            attn = jax.nn.softmax(scores, axis=-1)
            out = jnp.einsum('bkgls,bksd->bkgld', attn, v)
            out = out.transpose(0, 3, 1, 2, 4).reshape(b, l, H)
            out = out @ Wo + bo
            x = out + hidden_state
            mu = jnp.mean(x, axis=-1, keepdims=True)
            var = jnp.var(x, axis=-1, keepdims=True)
            return (x - mu) * jax.lax.rsqrt(var + EPS) * gamma + beta
        return _gqa_forward(hidden_state, encoder_hidden_state, encoder_attention_mask, Wq, bq, Wk, bk, Wv, bv, Wo, bo, gamma, beta)
    x = _L0_xattn_ref(x, ctx_2048, mask_Bx1xSxS2_ff0, L0_xattn_Wq, L0_xattn_bq, L0_xattn_Wk, L0_xattn_bk, L0_xattn_Wv, L0_xattn_bv, L0_xattn_Wo, L0_xattn_bo, L0_xattn_gamma, L0_xattn_beta)
    return x

_drawn_inputs = setup_inputs


def setup_inputs(seed=0):
    import zlib

    import numpy as np

    out = dict(_drawn_inputs(seed))
    spreads = {'L0_xattn_bq': (0.0, 0.8),
     'L0_xattn_bk': (0.0, 0.8),
     'L0_xattn_bv': (0.0, 0.1),
     'L0_xattn_bo': (0.0, 0.1),
     'L0_xattn_gamma': (1.0, 0.2),
     'L0_xattn_beta': (0.0, 0.1)}
    factors = {'L0_xattn_Wq': 7.578, 'L0_xattn_Wk': 7.452}
    for name, (base, spread) in spreads.items():
        noise = np.random.default_rng([zlib.crc32(name.encode()), seed]).standard_normal(out[name].shape)
        drawn = base * np.exp(spread * noise) if base else spread * noise
        out[name] = jnp.asarray(drawn.astype(out[name].dtype))
    for name, factor in factors.items():
        out[name] = (out[name] * factor).astype(out[name].dtype)
    return out
```

```python
from contextlib import ExitStack

import concourse.bass as bass
from concourse import mybir

F32 = mybir.dt.float32
F32R = mybir.dt.float32r
BF16 = mybir.dt.bfloat16
I32 = mybir.dt.int32
ALU = mybir.AluOpType
ACT = mybir.ActivationFunctionType
AX = mybir.AxisListType

P = 128
HD = 16
KVH = 8
GROUPS = 4
NH = KVH * GROUPS
EPS = 1e-6
SCALE = 0.25
PAIRS = [(0, 0), (1, 0), (2, 0), (0, 1), (1, 1), (0, 2)]
PARTS = 3
STACK = HD * len(PAIRS)
MROWS = STACK + PARTS

SLOTS = NH
QUADS = 8
GRPS = 4
PV_LAG = 5

AUX = {2: "x0", 3: "x1", 4: "x2", 5: "x3", 6: "k", 7: "v", 8: "vturn", 9: "q0", 10: "q1", 12: "q2", 13: "q3",
       15: "y0a", 16: "y0b", 18: "y1a", 19: "y1b", 28: "mturn"}
MAX_SLOTS = 26


def max_tiles(s):
    def until(n):
        return min(NH, -(-NH * n // MAX_SLOTS))
    return range(until(s), until(s + 1))


def due(eng, sem, count):
    if not isinstance(count, int) or count > 0:
        eng.wait_ge(sem, count)


def build(nc, x, ctx_in, mask, w_q, b_q, w_k, b_k, w_v, b_v, w_o, b_o, gamma, beta, out):
    NB, L, H = x.shape
    S = ctx_in.shape[1]
    LT, ST = L // P, S // P
    CH = H // P
    assert (LT, ST, CH, L, S) == (2, 2, 4, 256, 256) and NB % 2 == 0 and NB >= 6

    with ExitStack() as stack:
        def sb(name, shape, dt=F32):
            return stack.enter_context(nc.sbuf_tensor(name, shape, dt))

        def sem(name):
            return stack.enter_context(nc.semaphore(name))

        wq = [sb(f"wq_{n}", [P, CH, H], F32R) for n in "hl"]
        wo = [sb(f"wo_{n}", [P, CH, H], F32R) for n in "hl"]
        wk = [sb(f"wk_{n}", [P, CH, P], F32R) for n in "hl"]
        wv = [sb(f"wv_{n}", [P, CH, P], F32R) for n in "hl"]
        bias_q, bias_k, bias_v = sb("bias_q", [P, CH]), sb("bias_k", [P, 1]), sb("bias_v", [P, 1])
        gamma_row, beta_row, bo_row = sb("gamma_row", [P, H]), sb("beta_row", [P, H]), sb("bo_row", [P, H])
        ident, ident16 = sb("ident", [P, P]), sb("ident16", [P, P], BF16)
        ones = sb("ones", [P, 1])
        x_in, c_in = sb("x_in", [P, LT, H]), sb("c_in", [P, ST, H])
        turned = [[sb(f"{a}T_{n}", [P, CH, L], F32R) for n in "hl"] for a in "xc"]
        k_parts = sb("k_parts", [P, PARTS, S], BF16)
        k_rest = sb("k_rest", [P, S])
        q_parts = [sb(f"q_parts{h}", [P, PARTS, 2, L], BF16) for h in range(2)]
        q_rest = sb("q_rest", [P, 2, 2, L])
        v_rows = [sb(f"v_rows{u}", [P, S]) for u in range(2)]
        q_stack = [sb(f"q_stack{u}", [P, NH, L], BF16) for u in range(2)]
        k_stack = [sb(f"k_stack{u}", [P, KVH, S], BF16) for u in range(2)]
        v_ones = [sb(f"v_ones{u}", [P, ST, KVH, 2 * HD]) for u in range(2)]
        neg_max = sb("neg_max", [P, LT, GROUPS, KVH])
        neg_max_rest = sb("neg_max_rest", [P, LT * GROUPS, KVH])
        max_parts = sb("max_parts", [P, LT, GROUPS, PARTS, KVH], BF16)
        max_rows = sb("max_rows", [PARTS * KVH, GROUPS * L], BF16)
        probs = sb("probs", [P, 8, 512])
        sums_t = sb("sums_t", [P, 512])
        recip = sb("recip", [P, 16])
        attn_t = sb("attn_t", [P, 256])
        attn = [sb(f"attn{i}", [P, L]) for i in range(2)]
        attn_parts = [[sb(f"attn_{n}{u}", [P, GRPS, L], F32R) for n in "hl"] for u in range(2)]
        resid = sb("resid", [P, LT, H])
        normed = sb("normed", [P, LT, H])
        stats, mean_var = sb("stats", [P, LT, 6]), sb("mean_var", [P, LT, 2])
        rstd, shift, power = sb("rstd", [P, LT]), sb("shift", [P, LT]), sb("power", [P, LT])
        scan = sb("scan", [P, 4])
        flag = sb("flag", [1, 1], I32)
        mask_in = sb("mask_in", [P, LT, S])
        mask_t = [sb(f"mask_t{u}", [P, ST, L]) for u in range(2)]

        s1_bank = [stack.enter_context(nc.psum_tensor(f"s1_bank{i}", [P, 512], F32)) for i in range(2)]
        s2_bank = [stack.enter_context(nc.psum_tensor(f"s2_bank{i}", [P, 512], F32)) for i in range(2)]
        sum_bank = stack.enter_context(nc.psum_tensor("sum_bank", [P, 512], F32))
        bank = {n: stack.enter_context(nc.psum_tensor(f"bank_{n}", [P, 512], F32)) for n in "abc"}
        turn_bank = {0: bank["a"], 1: bank["b"], 2: bank["c"], 3: bank["a"]}
        q_bank = {0: bank["a"], 1: bank["b"]}
        y_bank = {0: bank["c"], 1: bank["a"]}

        q_scratch = nc.dram_tensor("q_scratch", [2, PARTS * 2, P, L], BF16)
        k_scratch = nc.dram_tensor("k_scratch", [PARTS, P, S], BF16)

        w_in = [sem(f"w_in{i}") for i in range(4)]
        biases_in, rows_in = sem("biases_in"), sem("rows_in")
        mask_scan_in = sem("mask_scan_in")
        x_loaded, c_loaded, resid_loaded = sem("x_loaded"), sem("c_loaded"), sem("resid_loaded")
        mask_loaded = sem("mask_loaded")
        k_out = sem("k_out")
        q_out = [sem(f"q_out{h}") for h in range(2)]
        stacked = [sem(f"stacked{h}") for h in range(2)]
        max_in = sem("max_in")
        y_out = sem("y_out")
        sp_passed, pool_passed, dve_passed = sem("sp_passed"), sem("pool_passed"), sem("dve_passed")
        consts = sem("consts")
        w_high, w_low = sem("w_high"), sem("w_low")
        bias_scaled = sem("bias_scaled")
        scanned, nonzero, flag_sum, flag_set = sem("scanned"), sem("nonzero"), sem("flag_sum"), sem("flag_set")
        turned_pe, proj_pe, vturn_pe = sem("turned_pe"), sem("proj_pe"), sem("vturn_pe")
        s1_ready, mturn_pe, s2_ready = sem("s1_ready"), sem("mturn_pe"), sem("s2_ready")
        pv_done, y_ready = sem("pv_done"), sem("y_ready")
        turned_high, proj_high, v_ready = sem("turned_high"), sem("proj_high"), sem("v_ready")
        max_rows_ready, exp_done, normed_act = sem("max_rows_ready"), sem("exp_done"), sem("normed_act")
        turned_low, rest_done, s1_used, max_split = sem("turned_low"), sem("rest_done"), sem("s1_used"), sem("max_split")
        sums_turned, recip_done, attn_scaled, attn_back = (sem(n) for n in ("sums_turned", "recip_done", "attn_scaled", "attn_back"))
        resid_added, norm_stats = sem("resid_added"), sem("norm_stats")
        s1_masked, s2_masked, mask_turned = sem("s1_masked"), sem("s2_masked"), sem("mask_turned")
        parts_mid, parts_done = sem("parts_mid"), sem("parts_done")
        attn_high, attn_low = sem("attn_high"), sem("attn_low")
        norm_factors = sem("norm_factors")
        resid_biased, gamma_done, out_ready = sem("resid_biased"), sem("gamma_done"), sem("out_ready")

        block = stack.enter_context(nc.Block())

        STEPS_BEFORE = range(-2, 2)
        LOOP_START, LOOP_END = 2, NB - 3
        STEPS_AFTER = range(NB - 2, NB + 1)

        def stages(t):
            if not isinstance(t, int):
                return True, True, True, True
            return 0 <= t + 2 < NB, 0 <= t + 1 < NB, 0 <= t < NB, 0 <= t - 1 < NB

        stage_wq = probs[:, 0:CH, :]
        stage_wo = probs[:, CH:2 * CH, :]
        stage_wk = resid[:, 0, :].rearrange("p (c n) -> p c n", c=CH)
        stage_wv = resid[:, 1, :].rearrange("p (c n) -> p c n", c=CH)
        scan_cols = NB * L * S // P // 2
        scan_part = [q_stack[i][:, :, :].rearrange("p h l -> p (h l)").bitcast(F32)[:, 0:scan_cols] for i in range(2)]

        @block.sync
        def _(sp):
            def rows(ap):
                return ap.rearrange("(t p) d -> p t d", p=P)

            def stack_half(b_parity, half):
                for j, (qp, kp) in enumerate(PAIRS):
                    sp.dma_start(q_stack[b_parity][HD * j:HD * (j + 1), 16 * half:16 * (half + 1), :],
                                 q_scratch[half, 2 * qp:2 * qp + 2].rearrange("m (h d) l -> d (m h) l", d=HD)).then_inc(stacked[half], 16)
                    sp.dma_start(k_stack[b_parity][HD * j:HD * (j + 1), 4 * half:4 * (half + 1), :],
                                 k_scratch[kp, 64 * half:64 * (half + 1)].rearrange("(h d) l -> d h l", d=HD)).then_inc(stacked[half], 16)

            def step(t, par, general):
                project, maxima, attend, output = stages(t)
                if project and (not isinstance(t, int) or t > -2):
                    sp.wait_ge(turned_pe, 4 * (t + 2))
                    sp.dma_start(x_in[:, :, :], rows(x[t + 2])).then_inc(x_loaded, 16)
                    sp.dma_start(c_in[:, :, :], rows(ctx_in[t + 2])).then_inc(c_loaded, 16)
                if maxima and general is not None:
                    with sp.If(general != 0):
                        due(sp, mask_turned, t + 1)
                        sp.dma_start(mask_in[:, :, :], rows(mask[t + 1, 0])).then_inc(mask_loaded, 16)
                if maxima:
                    due(sp, s2_ready, SLOTS * t)
                    sp.sem_inc(sp_passed)
                    sp.wait_ge(q_out[1], 16 * (t + 2))
                    stack_half(1 - par, 1)
                if output:
                    if isinstance(t, int):
                        sp.wait_ge(w_low, 4)
                    due(sp, normed_act, 2 * (t - 1))
                    sp.dma_start(resid[:, :, :], rows(x[t - 1])).then_inc(resid_loaded, 16)
                if project:
                    b2 = t + 2
                    sp.wait_ge(parts_done, 3 * b2 + 1)
                    for h in range(2):
                        sp.sem_inc(sp_passed)
                        due(sp, stacked[h], 192 * b2)
                    sp.dma_start(k_scratch.rearrange("m p l -> p m l"), k_parts[:, :, :]).then_inc(k_out, 16)
                    sp.wait_ge(parts_done, 3 * b2 + 2)
                    sp.dma_start(q_scratch[0].rearrange("m p l -> p m l"),
                                 q_parts[0][:, :, :, :].rearrange("p a m l -> p (a m) l")).then_inc(q_out[0], 16)
                    sp.wait_ge(parts_done, 3 * b2 + 3)
                    sp.dma_start(q_scratch[1].rearrange("m p l -> p m l"),
                                 q_parts[1][:, :, :, :].rearrange("p a m l -> p (a m) l")).then_inc(q_out[1], 16)
                    sp.wait_ge(k_out, 16 * (b2 + 1))
                    sp.sem_inc(sp_passed)
                    sp.wait_ge(q_out[0], 16 * (b2 + 1))
                    sp.sem_inc(sp_passed)
                    due(sp, s2_ready, SLOTS * t + SLOTS // 2)
                    if isinstance(t, int) and t < 0:
                        sp.wait_ge(scanned, t + 3)
                    stack_half(par, 0)
                if output:
                    sp.wait_ge(out_ready, 2 * t)
                    sp.dma_start(rows(out[t - 1]), normed[:, :, :]).then_inc(y_out, 16)
                if maxima:
                    sp.wait_ge(max_rows_ready, t + 2)
                    for part in range(PARTS):
                        sp.dma_start(q_stack[1 - par][STACK + part:STACK + part + 1, :, :].rearrange("o (k g) l -> o k (g l)", k=KVH),
                                     max_rows[part * KVH:(part + 1) * KVH, :]).then_inc(max_in, 16)

            sp.dma_start(x_in[:, :, :], rows(x[0])).then_inc(x_loaded, 16)
            sp.dma_start(c_in[:, :, :], rows(ctx_in[0])).then_inc(c_loaded, 16)
            for w, staged, s in ((w_k, stage_wk, w_in[1]), (w_v, stage_wv, w_in[2]), (w_q, stage_wq, w_in[0])):
                sp.dma_start(staged, w.rearrange("(c p) n -> p c n", p=P)).then_inc(s, 16)
            with nc.allow_non_contiguous_dma("biases, once"):
                sp.dma_start(bias_q[:, :], b_q.rearrange("(m p) -> p m", p=P)).then_inc(biases_in, 16)
                sp.dma_start(bias_k[:, :], b_k.rearrange("(p o) -> p o", o=1)).then_inc(biases_in, 16)
                sp.dma_start(bias_v[:, :], b_v.rearrange("(p o) -> p o", o=1)).then_inc(biases_in, 16)
            whole = mask.rearrange("b o l s -> (b o l s)").rearrange("(i p n) -> i p n", i=2, p=P)
            for i in range(2):
                sp.dma_start(scan_part[i], whole[i]).then_inc(mask_scan_in, 16)
            sp.dma_start(stage_wo, w_o.rearrange("(c p) n -> p c n", p=P)).then_inc(w_in[3], 16)
            for row, src in ((gamma_row, gamma), (beta_row, beta), (bo_row, b_o)):
                sp.dma_start(row[:, :], src.partition_broadcast(P)).then_inc(rows_in, 16)

            step(-2, 0, None)
            sp.wait_ge(flag_set, 1)
            general = sp.value_load(flag[0:1, 0:1], min_val=0, max_val=1)
            for t in STEPS_BEFORE[1:]:
                step(t, t % 2, general)
            with sp.Fori(LOOP_START, LOOP_END, 2) as t:
                step(t, 0, general)
                step(t + 1, 1, general)
            for t in STEPS_AFTER:
                step(t, t % 2, general)
            sp.wait_ge(y_out, 16 * NB)

        @block.gpsimd
        def _(pool):
            for i, m in enumerate((ident, ident16)):
                nc.gpsimd.memset(m[:, :], 0.0).then_inc(consts, 1)
                pool.wait_ge(consts, 2 * i + 1)
                nc.gpsimd.affine_select(out=m[:, :], in_=m[:, :], compare_op=ALU.not_equal, fill=1.0, base=0,
                                        pattern=[[-1, P]], channel_multiplier=1).then_inc(consts, 1)
            nc.gpsimd.memset(ones[:, :], 1.0).then_inc(consts, 1)
            nc.gpsimd.memset(power[:, :], -0.5).then_inc(consts, 1)
            for u in range(2):
                nc.gpsimd.memset(v_ones[u][:, :, :, HD:2 * HD], 1.0).then_inc(consts, 1)
            for u in range(2):
                pool.wait_ge(consts, 8 + u)
                nc.gpsimd.memset(k_stack[u][STACK:MROWS, :, :], 1.0).then_inc(consts, 1)
            pool.wait_ge(consts, 10)

            def split_parts(b2, n, first, parts, rest):
                pool.wait_ge(rest_done, 3 * b2 + n + 1)
                pool.sem_inc(pool_passed)
                due(pool, k_out if n == 0 else q_out[n - 1], 16 * b2)
                pool.sem_inc(pool_passed)
                nc.gpsimd.tensor_copy(parts(1), rest).then_inc(parts_mid, 1)
                pool.wait_ge(parts_mid, 3 * b2 + n + 1)
                nc.gpsimd.tensor_tensor(parts(2), rest, parts(1), ALU.subtract).then_inc(parts_done, 1)

            def split_attn(b, par, grp):
                pool.wait_ge(attn_back, 4 * b + grp + 1)
                if grp == 0:
                    pool.sem_inc(pool_passed)
                    due(pool, y_ready, 2 * (b - 1))
                pool.sem_inc(pool_passed)
                high, low = (attn_parts[par][i][:, grp, :] for i in range(2))
                nc.gpsimd.tensor_copy(high, attn[grp % 2][:, :]).then_inc(attn_high, 1)
                pool.wait_ge(attn_high, 4 * b + grp + 1)
                nc.gpsimd.tensor_tensor(low, attn[grp % 2][:, :], high.bitcast(F32), ALU.subtract).then_inc(attn_low, 1)

            def norm_scale(b):
                pool.wait_ge(norm_stats, 4 * b + 4)
                pool.sem_inc(pool_passed)
                nc.gpsimd.tensor_scalar(rstd[:, :], mean_var[:, :, 1], EPS, None, ALU.add).then_inc(norm_factors, 1)
                pool.wait_ge(norm_factors, 4 * b + 1)
                nc.gpsimd.tensor_tensor(rstd[:, :], rstd[:, :], power[:, :], ALU.pow).then_inc(norm_factors, 1)
                pool.wait_ge(norm_factors, 4 * b + 2)
                nc.gpsimd.tensor_tensor(shift[:, :], mean_var[:, :, 0], rstd[:, :], ALU.mult).then_inc(norm_factors, 1)
                pool.wait_ge(norm_factors, 4 * b + 3)
                pool.sem_inc(pool_passed)
                nc.gpsimd.tensor_scalar(shift[:, :], shift[:, :], -1.0, None, ALU.mult).then_inc(norm_factors, 1)

            def gamma_beta(b, lt):
                pool.wait_ge(normed_act, 2 * b + lt + 1)
                nc.gpsimd.tensor_tensor(normed[:, lt, :], normed[:, lt, :], gamma_row[:, :], ALU.mult).then_inc(gamma_done, 1)
                pool.wait_ge(gamma_done, 2 * b + lt + 1)
                nc.gpsimd.tensor_tensor(normed[:, lt, :], normed[:, lt, :], beta_row[:, :], ALU.add).then_inc(out_ready, 1)

            def step(t, par):
                project, maxima, attend, output = stages(t)
                if output:
                    split_attn(t - 1, 1 - par, 3)
                    pool.wait_ge(rows_in, 48)
                    pool.wait_ge(resid_loaded, 16 * t)
                    nc.gpsimd.tensor_tensor(resid[:, :, :], resid[:, :, :], bo_row[:, :].unsqueeze(1).broadcast_to([P, LT, H]),
                                            ALU.add).then_inc(resid_biased, 1)
                if project:
                    split_parts(t + 2, 0, True, lambda i: k_parts[:, i, :], k_rest[:, :])
                    split_parts(t + 2, 1, False, lambda i: q_parts[0][:, i, :, :], q_rest[:, 0, :, :])
                if attend:
                    split_attn(t, par, 0)
                if project:
                    split_parts(t + 2, 2, False, lambda i: q_parts[1][:, i, :, :], q_rest[:, 1, :, :])
                if output:
                    norm_scale(t - 1)
                    gamma_beta(t - 1, 0)
                if attend:
                    split_attn(t, par, 1)
                if output:
                    gamma_beta(t - 1, 1)
                if attend:
                    split_attn(t, par, 2)

            for t in STEPS_BEFORE:
                step(t, t % 2)
            with pool.Fori(LOOP_START, LOOP_END, 2) as t:
                step(t, 0)
                step(t + 1, 1)
            for t in STEPS_AFTER:
                step(t, t % 2)

        @block.tensor
        def _(pe):
            def turn(t, i):
                b2, src = t + 2, (x_in, c_in)[i // 2]
                if i == 0:
                    pe.wait_ge(x_loaded, 16 * (b2 + 1))
                    due(pe, resid_added, 2 * (t - 1))
                    due(pe, rest_done, 3 * b2)
                if i == 1:
                    due(pe, max_rows_ready, t + 1)
                if i == 2:
                    pe.wait_ge(c_loaded, 16 * (b2 + 1))
                    due(pe, v_ready, t + 1)
                if i == 3:
                    pe.wait_ge(turned_low, 4 * b2 + 1)
                for c in range(2):
                    for lt in range(LT):
                        f = 2 * (i % 2) + c
                        last = nc.tensor.transpose(turn_bank[i][:, c * L + lt * P:c * L + (lt + 1) * P],
                                                   src[:, lt, f * P:(f + 1) * P], ident[:, :])
                last.then_inc(turned_pe, 1)

            def project_rows(dst, w, cols, src, inc=None):
                for c in range(CH):
                    for a, b in ((0, 0), (0, 1), (1, 0)):
                        last = nc.tensor.matmul(dst, w[a][:, c, cols], src[b][:, c, :],
                                                start=(c == 0 and (a, b) == (0, 0)), stop=(c == CH - 1 and a == 1))
                if inc is not None:
                    last.then_inc(inc, 1)

            def y_half(b, par, lt, part):
                if part == 0:
                    pe.wait_ge(attn_low, 4 * (b + 1))
                    if lt == 0:
                        pe.wait_ge(w_low, 4)
                for c in range(2 * part, 2 * part + 2):
                    for m, n in ((0, 0), (0, 1), (1, 0)):
                        last = nc.tensor.matmul(y_bank[lt][:, :], attn_parts[par][m][:, c, lt * P:(lt + 1) * P], wo[n][:, c, :],
                                                start=(c == 0 and (m, n) == (0, 0)), stop=(c == CH - 1 and m == 1))
                if part == 1:
                    last.then_inc(y_ready, 1)

            def scores_for_max(b, par, head):
                if head % 16 == 0:
                    pe.wait_ge(stacked[head // 16], 192 * (b + 1))
                if not isinstance(b, int) or b > 0 or head >= 2:
                    pe.wait_ge(s1_used, NH * b + head - 1)
                for lt in range(LT):
                    last = nc.tensor.matmul(s1_bank[head % 2][:, lt * S:(lt + 1) * S],
                                            q_stack[par][0:STACK, head, lt * P:(lt + 1) * P],
                                            k_stack[par][0:STACK, head // GROUPS, :], start=True, stop=True)
                last.then_inc(s1_ready, 1)

            def scores(b, par, j):
                grp, st, kv, pair = j // 8, j // 4 % 2, j // 2 % 2, j % 2
                kvh = 2 * grp + kv
                head = kvh * GROUPS + 2 * pair
                if j == 0:
                    pe.wait_ge(max_in, 48 * (b + 1))
                if not isinstance(b, int) or b > 0 or j >= 2:
                    pe.wait_ge(exp_done, SLOTS * b + j - 1)
                nc.tensor.matmul(s2_bank[j % 2][:, :], k_stack[par][0:MROWS, kvh, st * P:(st + 1) * P],
                                 q_stack[par][0:MROWS, head:head + 2, :], start=True, stop=True).then_inc(s2_ready, 1)

            def weighted_sums(b, par, q):
                grp, st = q // 2, q % 2
                pe.wait_ge(exp_done, SLOTS * b + 4 * q + 4)
                if q == 0:
                    pe.wait_ge(v_ready, b + 1)
                if st == 0:
                    due(pe, sums_turned, 4 * b + grp)
                for c in range(4):
                    last = nc.tensor.matmul(sum_bank[32 * c:32 * (c + 1), :], v_ones[par][:, st, 2 * grp + c // 2, :],
                                            probs[:, 4 * (q % 2) + c, :], start=(st == 0), stop=(st == 1))
                last.then_inc(pv_done, 1)

            def aux(t, par, what):
                project, maxima, attend, output = stages(t)
                b2 = t + 2
                if what[0] == "x" and project:
                    turn(t, int(what[1]))
                if what == "k" and project:
                    pe.wait_ge(turned_low, 4 * b2 + 4)
                    project_rows(bank["b"][:, 0:S], wk, slice(0, P), turned[1])
                if what == "v" and project:
                    project_rows(bank["b"][:, S:2 * S], wv, slice(0, P), turned[1], proj_pe)
                if what == "vturn" and maxima:
                    if project:
                        pe.wait_ge(turned_low, 4 * b2 + 3)
                    else:
                        pe.wait_ge(resid_added, 2 * (t - 1))
                    pe.wait_ge(proj_high, 3 * (t + 1) + 1)
                    for st in range(ST):
                        last = nc.tensor.transpose(bank["c"][:, st * P:(st + 1) * P],
                                                   v_rows[1 - par][:, st * P:(st + 1) * P], ident[:, :])
                    last.then_inc(vturn_pe, 1)
                if what in ("q0", "q1", "q2", "q3") and project:
                    m = int(what[1])
                    if m == 2:
                        pe.wait_ge(rest_done, 3 * b2 + 1)
                    project_rows(q_bank[m // 2][:, m % 2 * L:(m % 2 + 1) * L], wq, slice(m * P, (m + 1) * P), turned[0],
                                 proj_pe if m % 2 else None)
                if what[0] == "y" and output:
                    lt, part = int(what[1]), "ab".index(what[2])
                    if part == 0 and lt == 0:
                        if maxima:
                            pe.wait_ge(v_ready, t + 2)
                        elif not isinstance(t, int) or t > 1:
                            pe.wait_ge(resid_added, 2 * (t - 1))
                    if part == 0 and lt == 1:
                        if project:
                            pe.wait_ge(rest_done, 3 * b2 + 2)
                        else:
                            pe.wait_ge(resid_added, 2 * (t - 1))
                    y_half(t - 1, 1 - par, lt, part)
                if what == "mturn" and maxima:
                    if project:
                        pe.wait_ge(rest_done, 3 * b2 + 3)
                    else:
                        pe.wait_ge(max_rows_ready, t + 1)
                    pe.wait_ge(max_split, 4 * (t + 2))
                    rows = bank["b"][:, :].bitcast(BF16)
                    for g in range(GROUPS):
                        for lt in range(LT):
                            last = nc.tensor.transpose(rows[0:PARTS * KVH, g * L + lt * P:g * L + (lt + 1) * P],
                                                       max_parts[:, lt, g, :, :].rearrange("p a k -> p (a k)"), ident16[:, :])
                    last.then_inc(mturn_pe, 1)

            def step(t, par):
                project, maxima, attend, output = stages(t)
                if output:
                    weighted_sums(t - 1, 1 - par, QUADS - 1)
                for s in range(SLOTS):
                    if attend:
                        scores(t, par, s)
                    if maxima:
                        for head in max_tiles(s):
                            scores_for_max(t + 1, 1 - par, head)
                    if attend and s >= PV_LAG and (s - PV_LAG) % 4 == 0:
                        weighted_sums(t, par, (s - PV_LAG) // 4)
                    if s in AUX:
                        if isinstance(t, int) and t == -2 and AUX[s] in ("k", "v", "q0"):
                            pe.wait_ge(w_low, {"k": 1, "v": 2, "q0": 3}[AUX[s]])
                        aux(t, par, AUX[s])

            pe.wait_ge(consts, 10)
            step(-2, 0)
            pe.wait_ge(nonzero, 1)
            nc.tensor.matmul(s1_bank[0][0:1, 0:1], scan[:, 3:4], ones[:, :], start=True, stop=True).then_inc(flag_sum, 1)
            pe.wait_ge(flag_set, 1)
            for t in STEPS_BEFORE[1:]:
                step(t, t % 2)
            with pe.Fori(LOOP_START, LOOP_END, 2) as t:
                step(t, 0)
                step(t + 1, 1)
            for t in STEPS_AFTER:
                step(t, t % 2)

        @block.scalar
        def _(act):
            def turned_to_parts(t, i):
                act.wait_ge(turned_pe, 4 * (t + 2) + i + 1)
                if i == 0:
                    due(act, proj_pe, 3 * (t + 2))
                nc.scalar.activation(turned[i // 2][0][:, 2 * (i % 2):2 * (i % 2) + 2, :],
                                     turn_bank[i][:, :].rearrange("p (c l) -> p c l", c=2), ACT.Copy).then_inc(turned_high, 1)

            def step(t, par, general):
                project, maxima, attend, output = stages(t)
                b2 = t + 2
                for s in range(SLOTS):
                    if attend:
                        act.wait_ge(s2_masked if general else s2_ready, SLOTS * t + s + 1)
                        if s % 4 == 0:
                            due(act, pv_done, QUADS * t + s // 4 - 1)
                        nc.scalar.activation(probs[:, s % 8, :], s2_bank[s % 2][:, :], ACT.Exp).then_inc(exp_done, 1)
                    what = AUX.get(s)
                    if what and what[0] == "x" and project:
                        turned_to_parts(t, int(what[1]))
                    if what == "v" and project:
                        act.wait_ge(proj_pe, 3 * b2 + 1)
                        due(act, k_out, 16 * b2)
                        nc.scalar.activation(k_parts[:, 0, :], bank["b"][:, 0:S], ACT.Identity, bias=bias_k[:, 0:1])
                        due(act, vturn_pe, b2 - 1)
                        nc.scalar.activation(v_rows[par][:, :], bank["b"][:, S:2 * S], ACT.Identity,
                                             bias=bias_v[:, 0:1]).then_inc(proj_high, 1)
                    if what == "vturn" and maxima:
                        act.wait_ge(vturn_pe, t + 2)
                        due(act, pv_done, QUADS * t)
                        nc.scalar.activation(v_ones[1 - par][:, :, :, 0:HD],
                                             bank["c"][:, 0:S].rearrange("p (s k d) -> p s k d", s=ST, k=KVH),
                                             ACT.Copy).then_inc(v_ready, 1)
                    if what in ("q1", "q3") and project:
                        half = int(what[1]) // 2
                        act.wait_ge(proj_pe, 3 * b2 + 2 + half)
                        due(act, q_out[half], 16 * b2)
                        for m in range(2):
                            last = nc.scalar.activation(q_parts[half][:, 0, m, :], q_bank[half][:, m * L:(m + 1) * L],
                                                        ACT.Identity, bias=bias_q[:, 2 * half + m:2 * half + m + 1])
                        last.then_inc(proj_high, 1)
                    if s in NORM_SLOTS and output:
                        lt = NORM_SLOTS.index(s)
                        act.wait_ge(norm_factors, 4 * t)
                        if lt == 0:
                            due(act, y_out, 16 * (t - 1))
                        nc.scalar.activation(normed[:, lt, :], resid[:, lt, :], ACT.Identity, bias=shift[:, lt:lt + 1],
                                             scale=rstd[:, lt:lt + 1]).then_inc(normed_act, 1)
                    if what == "mturn" and maxima:
                        act.wait_ge(mturn_pe, t + 2)
                        due(act, max_in, 48 * (t + 1))
                        nc.scalar.activation(max_rows[:, :], bank["b"][:, :].bitcast(BF16)[0:PARTS * KVH, :],
                                             ACT.Copy).then_inc(max_rows_ready, 1)

            act.wait_ge(biases_in, 48)
            nc.scalar.activation(bias_q[:, :], bias_q[:, :], ACT.Copy, scale=SCALE).then_inc(bias_scaled, 1)
            for i, (staged, w, scale) in enumerate(((stage_wk, wk, 1.0), (stage_wv, wv, 1.0), (stage_wq, wq, SCALE), (stage_wo, wo, 1.0))):
                if i < 3:
                    act.wait_ge(w_in[(1, 2, 0)[i]], 16)
                    nc.scalar.activation(w[0][:, :, :], staged, ACT.Copy, scale=scale).then_inc(w_high, 1)
            act.wait_ge(bias_scaled, 1)
            step(-2, 0, False)
            act.wait_ge(w_in[3], 16)
            nc.scalar.activation(wo[0][:, :, :], stage_wo, ACT.Copy).then_inc(w_high, 1)
            act.wait_ge(w_low, 4)
            act.wait_ge(flag_set, 1)
            flagged = act.value_load(flag[0:1, 0:1], min_val=0, max_val=1)

            def steps(general):
                for t in STEPS_BEFORE[1:]:
                    step(t, t % 2, general)
                with act.Fori(LOOP_START, LOOP_END, 2) as t:
                    step(t, 0, general)
                    step(t + 1, 1, general)
                for t in STEPS_AFTER:
                    step(t, t % 2, general)

            with act.If(flagged != 0):
                steps(True)
            with act.Else():
                steps(False)

        @block.vector
        def _(dve):
            def turned_to_parts(t, i):
                n = 4 * (t + 2) + i + 1
                dve.wait_ge(turned_high, n)
                cols = slice(2 * (i % 2), 2 * (i % 2) + 2)
                high, low = turned[i // 2]
                nc.vector.tensor_tensor(low[:, cols, :], turn_bank[i][:, :].rearrange("p (c l) -> p c l", c=2),
                                        high[:, cols, :].bitcast(F32), ALU.subtract).then_inc(turned_low, 1)

            def take_max(b, par, head, general):
                tile = s1_bank[head % 2][:, :].rearrange("p (t s) -> p t s", t=LT)
                dve.wait_ge(s1_ready, NH * b + head + 1)
                if general:
                    if head == 0:
                        dve.wait_ge(mask_loaded, 16 * (b + 1))
                    nc.vector.tensor_tensor(tile, tile, mask_in[:, :, :], ALU.add).then_inc(s1_masked, 1)
                    dve.wait_ge(s1_masked, NH * b + head + 1)
                nc.vector.tensor_reduce(neg_max[:, :, head % GROUPS, head // GROUPS], tile, AX.X, ALU.max,
                                        negate=True).then_inc(s1_used, 1)

            def add_mask(b, par, j):
                st = j // 4 % 2
                tile = s2_bank[j % 2][:, :].rearrange("p (h l) -> p h l", h=2)
                if j == 0:
                    dve.wait_ge(mask_turned, b + 1)
                dve.wait_ge(s2_ready, SLOTS * b + j + 1)
                nc.vector.tensor_tensor(tile, tile, mask_t[par][:, st, :].unsqueeze(1).broadcast_to([P, 2, L]),
                                        ALU.add).then_inc(s2_masked, 1)

            def turn_mask(b, par):
                for i in range(L // 32):
                    lt, r = i // 4, 32 * (i % 4)
                    for q in range(4):
                        src = mask_in[r:r + 32, lt, :].rearrange("p (t q s) -> p t q s", t=ST, q=4)[:, :, q, :]
                        last = nc.vector.transpose(mask_t[par][32 * q:32 * (q + 1), :, 32 * i:32 * (i + 1)], src)
                last.then_inc(mask_turned, 1)

            def rest_of(b2, n):
                dve.wait_ge(proj_high, 3 * b2 + n + 1)
                if n == 0:
                    due(dve, parts_done, 3 * b2)
                    nc.vector.scalar_tensor_tensor(k_rest[:, :], bank["b"][:, 0:S], bias_k[:, 0:1], k_parts[:, 0, :],
                                                   ALU.add, ALU.subtract).then_inc(rest_done, 1)
                else:
                    for m in range(2):
                        last = nc.vector.scalar_tensor_tensor(
                            q_rest[:, n - 1, m, :], q_bank[n - 1][:, m * L:(m + 1) * L], bias_q[:, 2 * (n - 1) + m:2 * (n - 1) + m + 1],
                            q_parts[n - 1][:, 0, m, :], ALU.add, ALU.subtract)
                    last.then_inc(rest_done, 1)

            def split_max(b, i):
                nm = neg_max[:, :, :, :].rearrange("p t g k -> p (t g) k")
                part = [max_parts[:, :, :, a, :].rearrange("p t g k -> p (t g) k") for a in range(PARTS)]
                if i == 0:
                    dve.wait_ge(s1_used, NH * (b + 1))
                    due(dve, mturn_pe, b)
                    op = nc.vector.tensor_copy(part[0], nm)
                else:
                    dve.wait_ge(max_split, 4 * b + i)
                if i == 1:
                    op = nc.vector.tensor_tensor(neg_max_rest[:, :, :], nm, part[0], ALU.subtract)
                if i == 2:
                    op = nc.vector.tensor_copy(part[1], neg_max_rest[:, :, :])
                if i == 3:
                    op = nc.vector.tensor_tensor(part[2], neg_max_rest[:, :, :], part[1], ALU.subtract)
                op.then_inc(max_split, 1)

            def finish_sums(b, grp, i):
                n = 4 * b + grp + 1
                if i == 0:
                    dve.wait_ge(pv_done, QUADS * b + 2 * grp + 2)
                    nc.vector.transpose(sums_t[:, :], sum_bank[:, :]).then_inc(sums_turned, 1)
                if i == 1:
                    dve.wait_ge(sums_turned, n)
                    nc.vector.reciprocal(recip[:, :], sums_t[:, :].rearrange("p (n r) -> p n r", r=32)[:, :, HD]).then_inc(recip_done, 1)
                if i == 2:
                    dve.wait_ge(recip_done, n)
                    nc.vector.tensor_tensor(attn_t[:, :].rearrange("p (n g d) -> p g n d", g=2, d=HD),
                                            sums_t[:, :].rearrange("p (g n r) -> p g n r", g=2, r=32)[:, :, :, 0:HD],
                                            recip[:, :].rearrange("p (g n) -> p g n", g=2).unsqueeze(3).broadcast_to([P, 2, 8, HD]),
                                            ALU.mult).then_inc(attn_scaled, 1)
                if i == 3:
                    dve.wait_ge(attn_scaled, n)
                    due(dve, attn_low, n - 2)
                    nc.vector.transpose(attn[grp % 2][:, :], attn_t[:, :]).then_inc(attn_back, 1)

            def norm(b, lt, i):
                n = 4 * b + 2 * lt
                if i == 0:
                    dve.wait_ge(y_ready, 2 * b + lt + 1)
                    if lt == 0:
                        dve.wait_ge(resid_biased, b + 1)
                    nc.vector.tensor_tensor(resid[:, lt, :], y_bank[lt][:, :], resid[:, lt, :], ALU.add).then_inc(resid_added, 1)
                if i == 1:
                    dve.wait_ge(resid_added, 2 * b + lt + 1)
                    nc.vector.bn_stats(stats[:, lt, :], resid[:, lt, :]).then_inc(norm_stats, 1)
                if i == 2:
                    dve.wait_ge(norm_stats, n + 1)
                    dve.sem_inc(dve_passed)
                    nc.vector.bn_aggr(mean_var[:, lt, :], stats[:, lt, :]).then_inc(norm_stats, 1)

            def step(t, par, general):
                project, maxima, attend, output = stages(t)
                for s in range(SLOTS):
                    if general and attend:
                        add_mask(t, par, s)
                    tiles = list(max_tiles(s)) if maxima else []
                    for k in range(2):
                        if k < len(tiles):
                            take_max(t + 1, 1 - par, tiles[k], general)
                        i = 2 * s + k
                        if output and i < 4:
                            finish_sums(t - 1, 3, i)
                        for grp in range(3):
                            if attend and 0 <= i - 2 * (PV_LAG + 4 + 1 + 8 * grp) < 4:
                                finish_sums(t, grp, i - 2 * (PV_LAG + 5 + 8 * grp))
                        if output:
                            for lt in range(LT):
                                if 0 <= i - 2 * Y_SLOTS[lt] < 3:
                                    norm(t - 1, lt, i - 2 * Y_SLOTS[lt])
                        if maxima and 0 <= i - 2 * MAX_SLOTS < 4:
                            split_max(t + 1, i - 2 * MAX_SLOTS)
                    what = AUX.get(s)
                    if what and what[0] == "x" and project:
                        turned_to_parts(t, int(what[1]))
                    if project and what in ("v", "q1", "q3"):
                        rest_of(t + 2, ("v", "q1", "q3").index(what))
                if general and maxima:
                    turn_mask(t + 1, 1 - par)

            for i, (staged, w, scale) in enumerate(((stage_wk, wk, 1.0), (stage_wv, wv, 1.0), (stage_wq, wq, SCALE))):
                dve.wait_ge(w_high, i + 1)
                nc.vector.scalar_tensor_tensor(w[1][:, :, :], staged, scale, w[0][:, :, :].bitcast(F32), ALU.mult, ALU.subtract).then_inc(w_low, 1)
            dve.wait_ge(bias_scaled, 1)
            step(-2, 0, False)
            dve.wait_ge(mask_scan_in, 32)
            for i in range(2):
                nc.vector.tensor_reduce(scan[:, i:i + 1], scan_part[i], AX.X, ALU.max, apply_absolute_value=True).then_inc(scanned, 1)
            dve.wait_ge(scanned, 2)
            nc.vector.tensor_tensor(scan[:, 2:3], scan[:, 0:1], scan[:, 1:2], ALU.max).then_inc(scanned, 1)
            dve.wait_ge(scanned, 3)
            nc.vector.tensor_scalar(scan[:, 3:4], scan[:, 2:3], 0.0, None, ALU.not_equal).then_inc(nonzero, 1)
            dve.wait_ge(flag_sum, 1)
            nc.vector.tensor_scalar(flag[:, :], s1_bank[0][0:1, 0:1], 0.0, None, ALU.is_gt).then_inc(flag_set, 1)
            dve.wait_ge(w_high, 4)
            nc.vector.scalar_tensor_tensor(wo[1][:, :, :], stage_wo, 1.0, wo[0][:, :, :].bitcast(F32), ALU.mult, ALU.subtract).then_inc(w_low, 1)
            dve.wait_ge(flag_set, 1)
            flagged = dve.value_load(flag[0:1, 0:1], min_val=0, max_val=1)

            def steps(general):
                for t in STEPS_BEFORE[1:]:
                    step(t, t % 2, general)
                with dve.Fori(LOOP_START, LOOP_END, 2) as t:
                    step(t, 0, general)
                    step(t + 1, 1, general)
                for t in STEPS_AFTER:
                    step(t, t % 2, general)

            with dve.If(flagged != 0):
                steps(True)
            with dve.Else():
                steps(False)


Y_SLOTS = (17, 20)
NORM_SLOTS = (24, 25)

_INS = ["x", "ctx_2048", "mask_Bx1xSxS2_ff0", "L0_xattn_Wq", "L0_xattn_bq", "L0_xattn_Wk", "L0_xattn_bk", "L0_xattn_Wv",
        "L0_xattn_bv", "L0_xattn_Wo", "L0_xattn_bo", "L0_xattn_gamma", "L0_xattn_beta"]


def kernel(**inputs):
    import numpy as np
    import concourse.bacc as bacc
    from concourse.bass_utils import run_bass_kernel_spmd

    nc = bacc.Bacc("TRN2", target_bir_lowering=False, num_devices=1)
    arrays, args = {}, []
    for name in _INS:
        a = np.ascontiguousarray(inputs[name])
        arrays[f"in_{name}"] = a
        args.append(nc.dram_tensor(f"in_{name}", a.shape, mybir.dt.from_np(a.dtype), kind="ExternalInput").ap())
    out = nc.dram_tensor("out_y", inputs["x"].shape, F32, kind="ExternalOutput").ap()
    build(nc, *args, out)
    r = run_bass_kernel_spmd(nc, [arrays], core_ids=[0])
    return r.results[0]["out_y"]
```

```python
from contextlib import ExitStack

import concourse.bass as bass
from concourse import mybir

F32 = mybir.dt.float32
F32R = mybir.dt.float32r
BF16 = mybir.dt.bfloat16
I32 = mybir.dt.int32
ALU = mybir.AluOpType
ACT = mybir.ActivationFunctionType
AX = mybir.AxisListType

P = 128
HD = 16
KVH = 8
GROUPS = 4
NH = KVH * GROUPS
EPS = 1e-6
SCALE = 0.25
PAIRS = [(0, 0), (1, 0), (2, 0), (0, 1), (1, 1), (0, 2)]
PARTS = 3
Q_FIRST, Q_SIZES = (0, 2, 3), (2, 1, 1)
STACK = HD * len(PAIRS)
MROWS = STACK + PARTS

SLOTS = 32
TILES = NH
QUADS = 8
GRPS = 4
TURNS = ("c0", "c1", "x0", "x1")
PV_LAG = 5

MAX_SLOTS = 28
ATTEND_FROM = 7
PE_SIDE = {0: ["c0"], 1: ["c1"], 2: ["x0"], 3: ["x1"], 5: ["k.0"], 6: ["k.1"], 7: ["v.0"], 8: ["v.1", "vturn"],
           9: ["q0.0"], 11: ["q0.1"], 12: ["q1.0", "q1.1"], 13: ["y0.0"], 14: ["y0.1"], 15: ["y0.2"], 16: ["y0.3"],
           17: ["y1.0"], 19: ["y1.1"], 21: ["y1.2", "y1.3"], 24: ["q2.0"], 25: ["q2.1"], 27: ["q3.0"],
           29: ["q3.1"], 30: ["mturn"]}
ACT_SIDE = {0: ["group2", "c0"], 1: ["c1"], 2: ["x0"], 3: ["x1"], 5: ["mid3"], 6: ["attn3"], 10: ["kv", "vturn"],
            11: ["mid0"], 13: ["group0"], 15: ["mid1"], 17: ["attn0"], 24: ["attn1"], 26: ["group1", "norm0"],
            28: ["mid2"], 29: ["norm1"], 30: ["attn2"], 31: ["mturn"]}
POOL_ORDER = ["c0", "c1", "x0", "rest3", "x1", "low3", "attn3", "rest0", "low0", "bias", "rest1", "low1", "attn0",
              "factors", "rest2", "attn1", "gamma0", "low2", "gamma1", "attn2"]
SUMS_FROM = {3: 3, 0: 30, 1: 40, 2: 54}
NORM_FROM = (36, 43)
SPLIT_FROM = 55


STACKED = 16 * 2 * PARTS


def max_tiles(s):
    return [h for h in range(NH) if h * MAX_SLOTS // NH == s]


def attend_tiles(s):
    return [j for j in range(TILES) if ATTEND_FROM + j * (SLOTS - ATTEND_FROM) // TILES == s]


def due(eng, sem, count):
    if not isinstance(count, int) or count > 0:
        eng.wait_ge(sem, count)


def build(nc, x, ctx_in, mask, w_q, b_q, w_k, b_k, w_v, b_v, w_o, b_o, gamma, beta, out):
    NB, L, H = x.shape
    S = ctx_in.shape[1]
    LT, ST = L // P, S // P
    CH = H // P
    assert (LT, ST, CH, L, S) == (2, 2, 4, 256, 256) and NB % 2 == 0 and NB >= 6

    with ExitStack() as stack:
        def sb(name, shape, dt=F32):
            return stack.enter_context(nc.sbuf_tensor(name, shape, dt))

        def sem(name):
            return stack.enter_context(nc.semaphore(name))

        wq = [sb(f"wq_{n}", [P, CH, H], F32R) for n in "hl"]
        wo = [sb(f"wo_{n}", [P, CH, H], F32R) for n in "hl"]
        wk = [sb(f"wk_{n}", [P, CH, P], F32R) for n in "hl"]
        wv = [sb(f"wv_{n}", [P, CH, P], F32R) for n in "hl"]
        bias_q, bias_k, bias_v = sb("bias_q", [P, CH]), sb("bias_k", [P, 1]), sb("bias_v", [P, 1])
        gamma_row, beta_row, bo_row = sb("gamma_row", [P, H]), sb("beta_row", [P, H]), sb("bo_row", [P, H])
        ident, ident16 = sb("ident", [P, P]), sb("ident16", [P, P], BF16)
        ones = sb("ones", [P, 1])
        x_in, c_in = sb("x_in", [P, LT, H]), sb("c_in", [P, ST, H])
        turned = [[sb(f"{a}T_{n}", [P, CH, L], F32R) for n in "hl"] for a in "cx"]
        k_parts = sb("k_parts", [P, PARTS, S], BF16)
        k_rest = sb("k_rest", [P, S])
        q_parts = [sb(f"q_parts{g}", [P, n, PARTS, L], BF16) for g, n in enumerate(Q_SIZES)]
        q_rest = sb("q_rest", [P, CH, L])
        turned_full = [sb(f"turned_full{u}", [P, 2, L]) for u in range(2)]
        v_rows = [sb(f"v_rows{u}", [P, S]) for u in range(2)]
        q_stack = [sb(f"q_stack{u}", [P, NH, L], BF16) for u in range(2)]
        k_stack = [sb(f"k_stack{u}", [P, KVH, S], BF16) for u in range(2)]
        v_ones = [sb(f"v_ones{u}", [P, ST, KVH, 2 * HD]) for u in range(2)]
        neg_max = sb("neg_max", [P, LT, GROUPS, KVH])
        neg_max_rest = sb("neg_max_rest", [P, LT * GROUPS, KVH])
        max_parts = sb("max_parts", [P, LT, GROUPS, PARTS, KVH], BF16)
        max_rows = sb("max_rows", [PARTS * KVH, GROUPS * L], BF16)
        probs = sb("probs", [P, 8, 512])
        sums_t = sb("sums_t", [P, 512])
        recip = sb("recip", [P, 16])
        attn_t = sb("attn_t", [P, 256])
        attn = [sb(f"attn{i}", [P, L]) for i in range(2)]
        attn_parts = [[sb(f"attn_{n}{u}", [P, GRPS, L], F32R) for n in "hl"] for u in range(2)]
        resid = sb("resid", [P, LT, H])
        normed = sb("normed", [P, LT, H])
        stats, mean_var = sb("stats", [P, LT, 6]), sb("mean_var", [P, LT, 2])
        rstd, shift, power = sb("rstd", [P, LT]), sb("shift", [P, LT]), sb("power", [P, LT])
        scan = sb("scan", [P, 4])
        flag = sb("flag", [1, 1], I32)
        mask_in = sb("mask_in", [P, LT, S])
        mask_t = [sb(f"mask_t{u}", [P, ST, L]) for u in range(2)]

        s1_bank = [stack.enter_context(nc.psum_tensor(f"s1_bank{i}", [P, 512], F32)) for i in range(2)]
        s2_bank = [stack.enter_context(nc.psum_tensor(f"s2_bank{i}", [P, 512], F32)) for i in range(2)]
        sum_bank = stack.enter_context(nc.psum_tensor("sum_bank", [P, 512], F32))
        bank = {n: stack.enter_context(nc.psum_tensor(f"bank_{n}", [P, 512], F32)) for n in "abc"}
        turn_bank = [bank[n] for n in "acac"]
        q_bank = {0: bank["a"], 1: bank["b"]}
        y_bank = {0: bank["c"], 1: bank["a"]}

        q_scratch = [nc.dram_tensor(f"q_scratch{g}", [n * PARTS, P, L], BF16) for g, n in enumerate(Q_SIZES)]
        k_scratch = nc.dram_tensor("k_scratch", [PARTS, P, S], BF16)

        w_in = [sem(f"w_in{i}") for i in range(4)]
        biases_in, rows_in = sem("biases_in"), sem("rows_in")
        mask_scan_in = sem("mask_scan_in")
        x_loaded, c_loaded, resid_loaded = sem("x_loaded"), sem("c_loaded"), sem("resid_loaded")
        mask_loaded = sem("mask_loaded")
        k_out = sem("k_out")
        q_out = [sem(f"q_out{g}") for g in range(3)]
        stacked = [sem(f"stacked{g}") for g in range(3)]
        max_in = sem("max_in")
        y_out = sem("y_out")
        sp_passed, pool_passed, dve_passed = sem("sp_passed"), sem("pool_passed"), sem("dve_passed")
        consts = sem("consts")
        w_high, w_low = sem("w_high"), sem("w_low")
        bias_scaled = sem("bias_scaled")
        scanned, nonzero, flag_sum, flag_set = sem("scanned"), sem("nonzero"), sem("flag_sum"), sem("flag_set")
        turned_pe, proj_pe, vturn_pe = sem("turned_pe"), sem("proj_pe"), sem("vturn_pe")
        s1_ready, mturn_pe, s2_ready = sem("s1_ready"), sem("mturn_pe"), sem("s2_ready")
        pv_done, y_ready = sem("pv_done"), sem("y_ready")
        turned_high, proj_high, v_ready = sem("turned_high"), sem("proj_high"), sem("v_ready")
        parts_mid = sem("parts_mid")
        max_rows_ready, exp_done, normed_act = sem("max_rows_ready"), sem("exp_done"), sem("normed_act")
        attn_high = sem("attn_high")
        s1_used, max_split = sem("s1_used"), sem("max_split")
        sums_turned, recip_done, attn_scaled, attn_back = (sem(n) for n in ("sums_turned", "recip_done", "attn_scaled", "attn_back"))
        resid_added, norm_stats = sem("resid_added"), sem("norm_stats")
        s1_masked, s2_masked, mask_turned = sem("s1_masked"), sem("s2_masked"), sem("mask_turned")
        turned_low, rest_done, parts_done, attn_low = sem("turned_low"), sem("rest_done"), sem("parts_done"), sem("attn_low")
        norm_factors = sem("norm_factors")
        resid_biased, gamma_done, out_ready = sem("resid_biased"), sem("gamma_done"), sem("out_ready")

        block = stack.enter_context(nc.Block())

        STEPS_BEFORE = range(-2, 2)
        LOOP_START, LOOP_END = 2, NB - 3
        STEPS_AFTER = range(NB - 2, NB + 1)

        def stages(t):
            if not isinstance(t, int):
                return True, True, True, True
            return 0 <= t + 2 < NB, 0 <= t + 1 < NB, 0 <= t < NB, 0 <= t - 1 < NB

        stage_wq = probs[:, 0:CH, :]
        stage_wo = probs[:, CH:2 * CH, :]
        stage_wk = resid[:, 0, :].rearrange("p (c n) -> p c n", c=CH)
        stage_wv = resid[:, 1, :].rearrange("p (c n) -> p c n", c=CH)
        scan_cols = NB * L * S // P // 2
        scan_part = [q_stack[i][:, :, :].rearrange("p h l -> p (h l)").bitcast(F32)[:, 0:scan_cols] for i in range(2)]

        @block.sync
        def _(sp):
            def rows(ap):
                return ap.rearrange("(t p) d -> p t d", p=P)

            def parts_out(b, g):
                sp.wait_ge(parts_done, 4 * b + g + 2)
                sp.sem_inc(sp_passed)
                due(sp, stacked[g], STACKED * b)
                sp.dma_start(q_scratch[g].rearrange("m p l -> p m l"),
                             q_parts[g][:, :, :, :].rearrange("p m a l -> p (m a) l")).then_inc(q_out[g], 16)

            def stack_group(b_parity, g):
                n, first = Q_SIZES[g], Q_FIRST[g]
                for kp in range(PARTS):
                    js = [j for j, pair in enumerate(PAIRS) if pair[1] == kp]
                    rows_of_pairs = slice(HD * js[0], HD * (js[-1] + 1))
                    sp.dma_start(q_stack[b_parity][rows_of_pairs, 8 * first:8 * (first + n), :].rearrange("r (m h) l -> r m (h l)", m=n),
                                 q_scratch[g].rearrange("(m a) (d h) l -> (a d) m (h l)", m=n, d=HD)[0:HD * len(js)]).then_inc(stacked[g], 16)
                    sp.dma_start(k_stack[b_parity][rows_of_pairs, 2 * first:2 * (first + n), :],
                                 k_scratch[kp].rearrange("(d h) l -> d h l", d=HD)[:, 2 * first:2 * (first + n), :]
                                 .unsqueeze(0).broadcast_to([len(js), HD, 2 * n, S])).then_inc(stacked[g], 16)

            def step(t, par, general):
                project, maxima, attend, output = stages(t)
                load = not isinstance(t, int) or t + 3 < NB
                if maxima:
                    due(sp, s2_ready, TILES * t)
                    sp.sem_inc(sp_passed)
                    sp.wait_ge(q_out[1], 16 * (t + 2))
                    stack_group(1 - par, 1)
                if maxima and general is not None:
                    with sp.If(general != 0):
                        due(sp, mask_turned, t + 1)
                        sp.dma_start(mask_in[:, :, :], rows(mask[t + 1, 0])).then_inc(mask_loaded, 16)
                if output:
                    if isinstance(t, int):
                        sp.wait_ge(w_low, 4)
                    due(sp, normed_act, 2 * (t - 1))
                    sp.dma_start(resid[:, :, :], rows(x[t - 1])).then_inc(resid_loaded, 16)
                if load:
                    sp.wait_ge(turned_pe, 4 * (t + 2) + 2)
                    sp.dma_start(c_in[:, :, :], rows(ctx_in[t + 3])).then_inc(c_loaded, 16)
                    sp.wait_ge(turned_pe, 4 * (t + 2) + 4)
                    sp.dma_start(x_in[:, :, :], rows(x[t + 3])).then_inc(x_loaded, 16)
                if maxima:
                    parts_out(t + 1, 2)
                if project:
                    b2 = t + 2
                    sp.wait_ge(parts_done, 4 * b2 + 1)
                    for g in range(3):
                        sp.sem_inc(sp_passed)
                        if g < 2:
                            due(sp, stacked[g], STACKED * b2)
                if maxima:
                    sp.wait_ge(q_out[2], 16 * (t + 2))
                    stack_group(1 - par, 2)
                if project:
                    due(sp, stacked[2], STACKED * b2)
                    sp.dma_start(k_scratch.rearrange("m p l -> p m l"), k_parts[:, :, :]).then_inc(k_out, 16)
                    parts_out(b2, 0)
                    sp.wait_ge(k_out, 16 * (b2 + 1))
                    sp.sem_inc(sp_passed)
                    sp.wait_ge(q_out[0], 16 * (b2 + 1))
                    sp.sem_inc(sp_passed)
                    due(sp, s2_ready, TILES * t + TILES // 2)
                    if isinstance(t, int) and t < 0:
                        sp.wait_ge(scanned, t + 3)
                    stack_group(par, 0)
                    parts_out(b2, 1)
                if maxima:
                    sp.wait_ge(max_rows_ready, t + 2)
                    sp.dma_start(q_stack[1 - par][STACK:MROWS, :, :].rearrange("a (k g) l -> a k (g l)", k=KVH),
                                 max_rows[:, :]).then_inc(max_in, 16)
                if output:
                    sp.wait_ge(out_ready, 2 * t)
                    sp.dma_start(rows(out[t - 1]), normed[:, :, :]).then_inc(y_out, 16)

            sp.dma_start(c_in[:, :, :], rows(ctx_in[0])).then_inc(c_loaded, 16)
            sp.dma_start(stage_wk, w_k.rearrange("(c p) n -> p c n", p=P)).then_inc(w_in[1], 16)
            sp.dma_start(stage_wv, w_v.rearrange("(c p) n -> p c n", p=P)).then_inc(w_in[2], 16)
            sp.dma_start(x_in[:, :, :], rows(x[0])).then_inc(x_loaded, 16)
            sp.dma_start(stage_wq, w_q.rearrange("(c p) n -> p c n", p=P)).then_inc(w_in[0], 16)
            with nc.allow_non_contiguous_dma("biases, once"):
                sp.dma_start(bias_q[:, :], b_q.rearrange("(m p) -> p m", p=P)).then_inc(biases_in, 16)
                sp.dma_start(bias_k[:, :], b_k.rearrange("(p o) -> p o", o=1)).then_inc(biases_in, 16)
                sp.dma_start(bias_v[:, :], b_v.rearrange("(p o) -> p o", o=1)).then_inc(biases_in, 16)
            whole = mask.rearrange("b o l s -> (b o l s)").rearrange("(i p n) -> i p n", i=2, p=P)
            for i in range(2):
                sp.dma_start(scan_part[i], whole[i]).then_inc(mask_scan_in, 16)
            sp.dma_start(stage_wo, w_o.rearrange("(c p) n -> p c n", p=P)).then_inc(w_in[3], 16)
            for row, src in ((gamma_row, gamma), (beta_row, beta), (bo_row, b_o)):
                sp.dma_start(row[:, :], src.partition_broadcast(P)).then_inc(rows_in, 16)

            step(-2, 0, None)
            sp.wait_ge(flag_set, 1)
            general = sp.value_load(flag[0:1, 0:1], min_val=0, max_val=1)
            for t in STEPS_BEFORE[1:]:
                step(t, t % 2, general)
            with sp.Fori(LOOP_START, LOOP_END - 2, 2) as t:
                step(t, 0, general)
                step(t + 1, 1, general)
            for t in range(NB - 4, NB + 1):
                step(t, t % 2, general)
            sp.wait_ge(y_out, 16 * NB)

        @block.gpsimd
        def _(pool):
            for i, m in enumerate((ident, ident16)):
                nc.gpsimd.memset(m[:, :], 0.0).then_inc(consts, 1)
                pool.wait_ge(consts, 2 * i + 1)
                nc.gpsimd.affine_select(out=m[:, :], in_=m[:, :], compare_op=ALU.not_equal, fill=1.0, base=0,
                                        pattern=[[-1, P]], channel_multiplier=1).then_inc(consts, 1)
            nc.gpsimd.memset(ones[:, :], 1.0).then_inc(consts, 1)
            nc.gpsimd.memset(power[:, :], -0.5).then_inc(consts, 1)
            for u in range(2):
                nc.gpsimd.memset(v_ones[u][:, :, :, HD:2 * HD], 1.0).then_inc(consts, 1)
            for u in range(2):
                pool.wait_ge(consts, 8 + u)
                nc.gpsimd.memset(k_stack[u][STACK:MROWS, :, :], 1.0).then_inc(consts, 1)
            pool.wait_ge(consts, 10)

            def turned_rest(t, i):
                pool.wait_ge(turned_high, 4 * (t + 2) + i + 1)
                cols = slice(2 * (i % 2), 2 * (i % 2) + 2)
                high, low = turned[i // 2]
                nc.gpsimd.tensor_tensor(low[:, cols, :], turned_full[i % 2][:, :, :], high[:, cols, :].bitcast(F32),
                                        ALU.subtract).then_inc(turned_low, 1)

            def full_and_parts(n):
                if n == 0:
                    return k_rest[:, :], [k_parts[:, a, :] for a in range(PARTS)]
                first, size = Q_FIRST[n - 1], Q_SIZES[n - 1]
                return q_rest[:, first:first + size, :], [q_parts[n - 1][:, :, a, :] for a in range(PARTS)]

            def parts_rest(b, n):
                rest, part = full_and_parts(n)
                pool.wait_ge(proj_high, 4 * b + n + 1)
                nc.gpsimd.tensor_tensor(rest, rest, part[0], ALU.subtract).then_inc(rest_done, 1)

            def parts_lowest(b, n):
                rest, part = full_and_parts(n)
                pool.wait_ge(parts_mid, 4 * b + n + 1)
                nc.gpsimd.tensor_tensor(part[2], rest, part[1], ALU.subtract).then_inc(parts_done, 1)

            def split_attn(b, par, grp):
                pool.wait_ge(attn_high, 4 * b + grp + 1)
                high, low = (attn_parts[par][i][:, grp, :] for i in range(2))
                nc.gpsimd.tensor_tensor(low, attn[grp % 2][:, :], high.bitcast(F32), ALU.subtract).then_inc(attn_low, 1)

            def norm_scale(b):
                pool.wait_ge(norm_stats, 4 * b + 4)
                pool.sem_inc(pool_passed)
                nc.gpsimd.tensor_scalar(rstd[:, :], mean_var[:, :, 1], EPS, None, ALU.add).then_inc(norm_factors, 1)
                pool.wait_ge(norm_factors, 4 * b + 1)
                nc.gpsimd.tensor_tensor(rstd[:, :], rstd[:, :], power[:, :], ALU.pow).then_inc(norm_factors, 1)
                pool.wait_ge(norm_factors, 4 * b + 2)
                nc.gpsimd.tensor_tensor(shift[:, :], mean_var[:, :, 0], rstd[:, :], ALU.mult).then_inc(norm_factors, 1)
                pool.wait_ge(norm_factors, 4 * b + 3)
                pool.sem_inc(pool_passed)
                nc.gpsimd.tensor_scalar(shift[:, :], shift[:, :], -1.0, None, ALU.mult).then_inc(norm_factors, 1)

            def gamma_beta(b, lt):
                pool.wait_ge(normed_act, 2 * b + lt + 1)
                nc.gpsimd.tensor_tensor(normed[:, lt, :], normed[:, lt, :], gamma_row[:, :], ALU.mult).then_inc(gamma_done, 1)
                pool.wait_ge(gamma_done, 2 * b + lt + 1)
                nc.gpsimd.tensor_tensor(normed[:, lt, :], normed[:, lt, :], beta_row[:, :], ALU.add).then_inc(out_ready, 1)

            def add_bias(b):
                pool.wait_ge(rows_in, 48)
                pool.wait_ge(resid_loaded, 16 * (b + 1))
                nc.gpsimd.tensor_tensor(resid[:, :, :], resid[:, :, :], bo_row[:, :].unsqueeze(1).broadcast_to([P, LT, H]),
                                        ALU.add).then_inc(resid_biased, 1)

            def step(t, par):
                project, maxima, attend, output = stages(t)
                for what in POOL_ORDER:
                    if what in TURNS and project:
                        turned_rest(t, TURNS.index(what))
                    if what in ("rest0", "rest1", "rest2") and project:
                        parts_rest(t + 2, int(what[4]))
                    if what in ("low0", "low1", "low2") and project:
                        parts_lowest(t + 2, int(what[3]))
                    if what == "rest3" and maxima:
                        parts_rest(t + 1, 3)
                    if what == "low3" and maxima:
                        parts_lowest(t + 1, 3)
                    if what == "attn3" and output:
                        split_attn(t - 1, 1 - par, 3)
                    if what in ("attn0", "attn1", "attn2") and attend:
                        split_attn(t, par, int(what[4]))
                    if what == "bias" and output:
                        add_bias(t - 1)
                    if what == "factors" and output:
                        norm_scale(t - 1)
                    if what in ("gamma0", "gamma1") and output:
                        gamma_beta(t - 1, int(what[5]))

            for t in STEPS_BEFORE:
                step(t, t % 2)
            with pool.Fori(LOOP_START, LOOP_END, 2) as t:
                step(t, 0)
                step(t + 1, 1)
            for t in STEPS_AFTER:
                step(t, t % 2)

        @block.tensor
        def _(pe):
            def turn(t, i):
                b2, src = t + 2, (c_in, x_in)[i // 2]
                if i == 0:
                    pe.wait_ge(c_loaded, 16 * (b2 + 1))
                    due(pe, resid_added, 2 * (t - 1))
                    due(pe, proj_high, 4 * (b2 - 1) + 2)
                if i == 1:
                    due(pe, max_rows_ready, t + 1)
                if i == 2:
                    pe.wait_ge(x_loaded, 16 * (b2 + 1))
                if i >= 2:
                    pe.wait_ge(turned_high, 4 * b2 + i - 1)
                for c in range(2):
                    for lt in range(LT):
                        f = 2 * (i % 2) + c
                        last = nc.tensor.transpose(turn_bank[i][:, c * L + lt * P:c * L + (lt + 1) * P],
                                                   src[:, lt, f * P:(f + 1) * P], ident[:, :])
                last.then_inc(turned_pe, 1)

            def project_half(dst, w, cols, src, half, inc=None):
                for c in range(half * CH // 2, (half + 1) * CH // 2):
                    for a, b in ((0, 0), (0, 1), (1, 0)):
                        last = nc.tensor.matmul(dst, w[a][:, c, cols], src[b][:, c, :],
                                                start=(c == 0 and (a, b) == (0, 0)), stop=(c == CH - 1 and a == 1))
                if inc is not None and half == 1:
                    last.then_inc(inc, 1)

            def y_chunk(b, par, lt, c):
                for m, n in ((0, 0), (0, 1), (1, 0)):
                    last = nc.tensor.matmul(y_bank[lt][:, :], attn_parts[par][m][:, c, lt * P:(lt + 1) * P], wo[n][:, c, :],
                                            start=(c == 0 and (m, n) == (0, 0)), stop=(c == CH - 1 and m == 1))
                if c == CH - 1:
                    last.then_inc(y_ready, 1)

            def scores_for_max(b, par, head):
                if head in (8 * m for m in Q_FIRST):
                    pe.wait_ge(stacked[Q_FIRST.index(head // 8)], STACKED * (b + 1))
                if not isinstance(b, int) or b > 0 or head >= 2:
                    pe.wait_ge(s1_used, NH * b + head - 1)
                for lt in range(LT):
                    last = nc.tensor.matmul(s1_bank[head % 2][:, lt * S:(lt + 1) * S],
                                            q_stack[par][0:STACK, head, lt * P:(lt + 1) * P],
                                            k_stack[par][0:STACK, head // GROUPS, :], start=True, stop=True)
                last.then_inc(s1_ready, 1)

            def scores(b, par, j):
                grp, st, kv, pair = j // 8, j // 4 % 2, j // 2 % 2, j % 2
                kvh = 2 * grp + kv
                head = kvh * GROUPS + 2 * pair
                if j == 0:
                    pe.wait_ge(max_in, 16 * (b + 1))
                if not isinstance(b, int) or b > 0 or j >= 2:
                    pe.wait_ge(exp_done, TILES * b + j - 1)
                nc.tensor.matmul(s2_bank[j % 2][:, :], k_stack[par][0:MROWS, kvh, st * P:(st + 1) * P],
                                 q_stack[par][0:MROWS, head:head + 2, :], start=True, stop=True).then_inc(s2_ready, 1)

            def weighted_sums(b, par, q):
                grp, st = q // 2, q % 2
                pe.wait_ge(exp_done, TILES * b + 4 * q + 4)
                if q == 0:
                    pe.wait_ge(v_ready, b + 1)
                if st == 0:
                    due(pe, sums_turned, 4 * b + grp)
                for c in range(4):
                    last = nc.tensor.matmul(sum_bank[32 * c:32 * (c + 1), :], v_ones[par][:, st, 2 * grp + c // 2, :],
                                            probs[:, 4 * (q % 2) + c, :], start=(st == 0), stop=(st == 1))
                last.then_inc(pv_done, 1)

            def side(t, par, what):
                project, maxima, attend, output = stages(t)
                b2 = t + 2
                what, part = what.split(".") if "." in what else (what, "0")
                part = int(part)
                if what in TURNS and project:
                    turn(t, TURNS.index(what))
                if what == "k" and project:
                    if part == 0:
                        pe.wait_ge(turned_low, 4 * b2 + 2)
                        due(pe, proj_high, 4 * b2)
                        if isinstance(t, int) and t == -2:
                            pe.wait_ge(w_low, 1)
                    project_half(bank["b"][:, 0:S], wk, slice(0, P), turned[0], part)
                if what == "v" and project:
                    if part == 0 and isinstance(t, int) and t == -2:
                        pe.wait_ge(w_low, 2)
                    project_half(bank["b"][:, S:2 * S], wv, slice(0, P), turned[0], part, proj_pe)
                if what == "vturn" and maxima:
                    if project:
                        pe.wait_ge(turned_high, 4 * b2 + 4)
                    else:
                        pe.wait_ge(max_rows_ready, t + 1)
                    pe.wait_ge(proj_high, 4 * (t + 1) + 1)
                    for st in range(ST):
                        last = nc.tensor.transpose(bank["c"][:, st * P:(st + 1) * P],
                                                   v_rows[1 - par][:, st * P:(st + 1) * P], ident[:, :])
                    last.then_inc(vturn_pe, 1)
                if what[0] == "q" and project:
                    m, b = int(what[1]), t + 2
                    if part == 0 and m == 0:
                        pe.wait_ge(turned_low, 4 * b + 4)
                        if isinstance(t, int) and t == -2:
                            pe.wait_ge(w_low, 3)
                    if part == 0 and m == 3:
                        pe.wait_ge(proj_high, 4 * b + 3)
                    if part == 0 and m == 2:
                        pe.wait_ge(proj_high, 4 * b + 1)
                    project_half(q_bank[m // 2][:, m % 2 * L:(m % 2 + 1) * L], wq, slice(m * P, (m + 1) * P), turned[1],
                                 part, proj_pe if m > 0 else None)
                if what[0] == "y" and output:
                    lt = int(what[1])
                    if part == 0 and lt == 0:
                        pe.wait_ge(attn_low, 4 * t)
                        pe.wait_ge(w_low, 4)
                        if maxima:
                            pe.wait_ge(v_ready, t + 2)
                        else:
                            pe.wait_ge(resid_added, 2 * (t - 1))
                            pe.wait_ge(max_rows_ready, NB)
                    if part == 0 and lt == 1:
                        if project:
                            pe.wait_ge(proj_high, 4 * b2 + 2)
                        else:
                            pe.wait_ge(resid_added, 2 * (t - 1))
                    y_chunk(t - 1, 1 - par, lt, part)
                if what == "mturn" and maxima:
                    if output:
                        pe.wait_ge(resid_added, 2 * (t - 1) + 1)
                    else:
                        pe.wait_ge(v_ready, t + 2)
                    pe.wait_ge(max_split, 4 * (t + 2))
                    rows = bank["c"][:, :].bitcast(BF16)
                    for g in range(GROUPS):
                        for lt in range(LT):
                            last = nc.tensor.transpose(rows[0:PARTS * KVH, g * L + lt * P:g * L + (lt + 1) * P],
                                                       max_parts[:, lt, g, :, :].rearrange("p a k -> p (a k)"), ident16[:, :])
                    last.then_inc(mturn_pe, 1)

            def step(t, par):
                project, maxima, attend, output = stages(t)
                if output:
                    weighted_sums(t - 1, 1 - par, QUADS - 1)
                for s in range(SLOTS):
                    attend_now = attend_tiles(s) if attend else []
                    max_now = max_tiles(s) if maxima else []
                    for i in range(2):
                        for j in attend_now[i:i + 1]:
                            scores(t, par, j)
                            if j >= PV_LAG and (j - PV_LAG) % 4 == 0:
                                weighted_sums(t, par, (j - PV_LAG) // 4)
                        for head in max_now[i:i + 1]:
                            scores_for_max(t + 1, 1 - par, head)
                    for what in PE_SIDE.get(s, []):
                        side(t, par, what)

            pe.wait_ge(consts, 10)
            step(-2, 0)
            pe.wait_ge(nonzero, 1)
            nc.tensor.matmul(s1_bank[0][0:1, 0:1], scan[:, 3:4], ones[:, :], start=True, stop=True).then_inc(flag_sum, 1)
            pe.wait_ge(flag_set, 1)
            for t in STEPS_BEFORE[1:]:
                step(t, t % 2)
            with pe.Fori(LOOP_START, LOOP_END, 2) as t:
                step(t, 0)
                step(t + 1, 1)
            for t in STEPS_AFTER:
                step(t, t % 2)

        @block.scalar
        def _(act):
            def turned_out(t, i):
                act.wait_ge(turned_pe, 4 * (t + 2) + i + 1)
                if i == 0:
                    due(act, proj_pe, 4 * (t + 1) + 1)
                if i == 2:
                    due(act, proj_pe, 4 * (t + 2))
                due(act, turned_low, 4 * (t + 2) + i - 1)
                src = turn_bank[i][:, :].rearrange("p (c l) -> p c l", c=2)
                nc.scalar.activation(turned[i // 2][0][:, 2 * (i % 2):2 * (i % 2) + 2, :], src, ACT.Copy)
                nc.scalar.activation(turned_full[i % 2][:, :, :], src, ACT.Copy).then_inc(turned_high, 1)

            def exp_tile(t, j, general):
                act.wait_ge(s2_masked if general else s2_ready, TILES * t + j + 1)
                if j % 4 == 0:
                    due(act, pv_done, QUADS * t + j // 4 - 1)
                nc.scalar.activation(probs[:, j % 8, :], s2_bank[j % 2][:, :], ACT.Exp).then_inc(exp_done, 1)

            def q_group_out(b, g):
                act.wait_ge(proj_pe, 4 * b + 2 + g)
                due(act, q_out[g], 16 * b)
                for i in range(Q_SIZES[g]):
                    m = Q_FIRST[g] + i
                    src, bias = q_bank[m // 2][:, m % 2 * L:(m % 2 + 1) * L], bias_q[:, m:m + 1]
                    nc.scalar.activation(q_parts[g][:, i, 0, :], src, ACT.Identity, bias=bias)
                    last = nc.scalar.activation(q_rest[:, m, :], src, ACT.Identity, bias=bias)
                last.then_inc(proj_high, 1)

            def middle(b, n):
                act.wait_ge(rest_done, 4 * b + n + 1)
                if n == 0:
                    dst, rest = k_parts[:, 1, :], k_rest[:, :]
                else:
                    first, size = Q_FIRST[n - 1], Q_SIZES[n - 1]
                    dst, rest = q_parts[n - 1][:, :, 1, :], q_rest[:, first:first + size, :]
                nc.scalar.activation(dst, rest, ACT.Copy).then_inc(parts_mid, 1)

            def attn_out(b, par, grp):
                act.wait_ge(attn_back, 4 * b + grp + 1)
                if grp == 0:
                    due(act, y_ready, 2 * (b - 1))
                nc.scalar.activation(attn_parts[par][0][:, grp, :], attn[grp % 2][:, :], ACT.Copy).then_inc(attn_high, 1)

            def side(t, par, what):
                project, maxima, attend, output = stages(t)
                if what in TURNS and project:
                    turned_out(t, TURNS.index(what))
                if what == "kv" and project:
                    b2 = t + 2
                    act.wait_ge(proj_pe, 4 * b2 + 1)
                    due(act, k_out, 16 * b2)
                    nc.scalar.activation(k_parts[:, 0, :], bank["b"][:, 0:S], ACT.Identity, bias=bias_k[:, 0:1])
                    nc.scalar.activation(k_rest[:, :], bank["b"][:, 0:S], ACT.Identity, bias=bias_k[:, 0:1])
                    due(act, vturn_pe, b2 - 1)
                    nc.scalar.activation(v_rows[par][:, :], bank["b"][:, S:2 * S], ACT.Identity,
                                         bias=bias_v[:, 0:1]).then_inc(proj_high, 1)
                if what == "vturn" and maxima:
                    act.wait_ge(vturn_pe, t + 2)
                    due(act, pv_done, QUADS * t)
                    nc.scalar.activation(v_ones[1 - par][:, :, :, 0:HD],
                                         bank["c"][:, 0:S].rearrange("p (s k d) -> p s k d", s=ST, k=KVH),
                                         ACT.Copy).then_inc(v_ready, 1)
                if what in ("group0", "group1") and project:
                    q_group_out(t + 2, int(what[5]))
                if what == "group2" and maxima:
                    q_group_out(t + 1, 2)
                if what in ("mid0", "mid1", "mid2") and project:
                    middle(t + 2, int(what[3]))
                if what == "mid3" and maxima:
                    middle(t + 1, 3)
                if what in ("attn0", "attn1", "attn2") and attend:
                    attn_out(t, par, int(what[4]))
                if what == "attn3" and output:
                    attn_out(t - 1, 1 - par, 3)
                if what in ("norm0", "norm1") and output:
                    lt = int(what[4])
                    act.wait_ge(norm_factors, 4 * t)
                    if lt == 0:
                        due(act, y_out, 16 * (t - 1))
                    nc.scalar.activation(normed[:, lt, :], resid[:, lt, :], ACT.Identity, bias=shift[:, lt:lt + 1],
                                         scale=rstd[:, lt:lt + 1]).then_inc(normed_act, 1)
                if what == "mturn" and maxima:
                    act.wait_ge(mturn_pe, t + 2)
                    due(act, max_in, 16 * (t + 1))
                    nc.scalar.activation(max_rows[:, :], bank["c"][:, :].bitcast(BF16)[0:PARTS * KVH, :],
                                         ACT.Copy).then_inc(max_rows_ready, 1)

            def weight_high(i, staged, w, scale=1.0):
                act.wait_ge(w_in[i], 16)
                nc.scalar.activation(w[0][:, :, :], staged, ACT.Copy, scale=scale).then_inc(w_high, 1)

            def step(t, par, general):
                attend = stages(t)[2]
                for s in range(SLOTS):
                    if isinstance(t, int) and t == -2:
                        if "x0" in ACT_SIDE.get(s, []):
                            weight_high(1, stage_wk, wk)
                            weight_high(2, stage_wv, wv)
                        if "kv" in ACT_SIDE.get(s, []):
                            weight_high(0, stage_wq, wq, SCALE)
                            act.wait_ge(biases_in, 48)
                            nc.scalar.activation(bias_q[:, :], bias_q[:, :], ACT.Copy, scale=SCALE).then_inc(bias_scaled, 1)
                            act.wait_ge(bias_scaled, 1)
                    for j in attend_tiles(s) if attend else []:
                        exp_tile(t, j, general)
                    for what in ACT_SIDE.get(s, []):
                        side(t, par, what)

            step(-2, 0, False)
            weight_high(3, stage_wo, wo)
            act.wait_ge(w_low, 4)
            act.wait_ge(flag_set, 1)
            flagged = act.value_load(flag[0:1, 0:1], min_val=0, max_val=1)

            def steps(general):
                for t in STEPS_BEFORE[1:]:
                    step(t, t % 2, general)
                with act.Fori(LOOP_START, LOOP_END, 2) as t:
                    step(t, 0, general)
                    step(t + 1, 1, general)
                for t in STEPS_AFTER:
                    step(t, t % 2, general)

            with act.If(flagged != 0):
                steps(True)
            with act.Else():
                steps(False)

        @block.vector
        def _(dve):
            def take_max(b, par, head, general):
                tile = s1_bank[head % 2][:, :].rearrange("p (t s) -> p t s", t=LT)
                dve.wait_ge(s1_ready, NH * b + head + 1)
                if general:
                    if head == 0:
                        dve.wait_ge(mask_loaded, 16 * (b + 1))
                    nc.vector.tensor_tensor(tile, tile, mask_in[:, :, :], ALU.add).then_inc(s1_masked, 1)
                    dve.wait_ge(s1_masked, NH * b + head + 1)
                nc.vector.tensor_reduce(neg_max[:, :, head % GROUPS, head // GROUPS], tile, AX.X, ALU.max,
                                        negate=True).then_inc(s1_used, 1)

            def add_mask(b, par, j):
                st = j // 4 % 2
                tile = s2_bank[j % 2][:, :].rearrange("p (h l) -> p h l", h=2)
                if j == 0:
                    dve.wait_ge(mask_turned, b + 1)
                dve.wait_ge(s2_ready, TILES * b + j + 1)
                nc.vector.tensor_tensor(tile, tile, mask_t[par][:, st, :].unsqueeze(1).broadcast_to([P, 2, L]),
                                        ALU.add).then_inc(s2_masked, 1)

            def turn_mask(b, par):
                for i in range(L // 32):
                    lt, r = i // 4, 32 * (i % 4)
                    for q in range(4):
                        src = mask_in[r:r + 32, lt, :].rearrange("p (t q s) -> p t q s", t=ST, q=4)[:, :, q, :]
                        last = nc.vector.transpose(mask_t[par][32 * q:32 * (q + 1), :, 32 * i:32 * (i + 1)], src)
                last.then_inc(mask_turned, 1)

            def split_max(b, i):
                nm = neg_max[:, :, :, :].rearrange("p t g k -> p (t g) k")
                part = [max_parts[:, :, :, a, :].rearrange("p t g k -> p (t g) k") for a in range(PARTS)]
                if i == 0:
                    dve.wait_ge(s1_used, NH * (b + 1))
                    due(dve, mturn_pe, b)
                    op = nc.vector.tensor_copy(part[0], nm)
                else:
                    dve.wait_ge(max_split, 4 * b + i)
                if i == 1:
                    op = nc.vector.tensor_tensor(neg_max_rest[:, :, :], nm, part[0], ALU.subtract)
                if i == 2:
                    op = nc.vector.tensor_copy(part[1], neg_max_rest[:, :, :])
                if i == 3:
                    op = nc.vector.tensor_tensor(part[2], neg_max_rest[:, :, :], part[1], ALU.subtract)
                op.then_inc(max_split, 1)

            def finish_sums(b, grp, i):
                n = 4 * b + grp + 1
                if i == 0:
                    dve.wait_ge(pv_done, QUADS * b + 2 * grp + 2)
                    nc.vector.transpose(sums_t[:, :], sum_bank[:, :]).then_inc(sums_turned, 1)
                if i == 1:
                    dve.wait_ge(sums_turned, n)
                    nc.vector.reciprocal(recip[:, :], sums_t[:, :].rearrange("p (n r) -> p n r", r=32)[:, :, HD]).then_inc(recip_done, 1)
                if i == 2:
                    dve.wait_ge(recip_done, n)
                    nc.vector.tensor_tensor(attn_t[:, :].rearrange("p (n g d) -> p g n d", g=2, d=HD),
                                            sums_t[:, :].rearrange("p (g n r) -> p g n r", g=2, r=32)[:, :, :, 0:HD],
                                            recip[:, :].rearrange("p (g n) -> p g n", g=2).unsqueeze(3).broadcast_to([P, 2, 8, HD]),
                                            ALU.mult).then_inc(attn_scaled, 1)
                if i == 3:
                    dve.wait_ge(attn_scaled, n)
                    due(dve, attn_low, n - 2)
                    nc.vector.transpose(attn[grp % 2][:, :], attn_t[:, :]).then_inc(attn_back, 1)

            def norm(b, lt, i):
                n = 4 * b + 2 * lt
                if i == 0:
                    dve.wait_ge(y_ready, 2 * b + lt + 1)
                    if lt == 0:
                        dve.wait_ge(resid_biased, b + 1)
                    nc.vector.tensor_tensor(resid[:, lt, :], y_bank[lt][:, :], resid[:, lt, :], ALU.add).then_inc(resid_added, 1)
                if i == 1:
                    dve.wait_ge(resid_added, 2 * b + lt + 1)
                    nc.vector.bn_stats(stats[:, lt, :], resid[:, lt, :]).then_inc(norm_stats, 1)
                if i == 2:
                    dve.wait_ge(norm_stats, n + 1)
                    dve.sem_inc(dve_passed)
                    nc.vector.bn_aggr(mean_var[:, lt, :], stats[:, lt, :]).then_inc(norm_stats, 1)

            def step(t, par, general):
                project, maxima, attend, output = stages(t)
                for s in range(SLOTS):
                    attend_now = attend_tiles(s) if attend and general else []
                    max_now = max_tiles(s) if maxima else []
                    for k in range(2):
                        for j in attend_now[k:k + 1]:
                            add_mask(t, par, j)
                        for head in max_now[k:k + 1]:
                            take_max(t + 1, 1 - par, head, general)
                        i = 2 * s + k
                        for grp, start in SUMS_FROM.items():
                            if 0 <= i - start < 4:
                                if grp == 3 and output:
                                    finish_sums(t - 1, 3, i - start)
                                if grp < 3 and attend:
                                    finish_sums(t, grp, i - start)
                        if output:
                            for lt in range(LT):
                                if 0 <= i - NORM_FROM[lt] < 3:
                                    norm(t - 1, lt, i - NORM_FROM[lt])
                        if maxima and 0 <= i - SPLIT_FROM < 4:
                            split_max(t + 1, i - SPLIT_FROM)
                if general and maxima:
                    turn_mask(t + 1, 1 - par)

            for i, (staged, w, scale) in enumerate(((stage_wk, wk, 1.0), (stage_wv, wv, 1.0), (stage_wq, wq, SCALE))):
                dve.wait_ge(w_high, i + 1)
                nc.vector.scalar_tensor_tensor(w[1][:, :, :], staged, scale, w[0][:, :, :].bitcast(F32), ALU.mult, ALU.subtract).then_inc(w_low, 1)
            dve.wait_ge(mask_scan_in, 32)
            for i in range(2):
                nc.vector.tensor_reduce(scan[:, i:i + 1], scan_part[i], AX.X, ALU.max, apply_absolute_value=True).then_inc(scanned, 1)
            dve.wait_ge(scanned, 2)
            nc.vector.tensor_tensor(scan[:, 2:3], scan[:, 0:1], scan[:, 1:2], ALU.max).then_inc(scanned, 1)
            dve.wait_ge(scanned, 3)
            nc.vector.tensor_scalar(scan[:, 3:4], scan[:, 2:3], 0.0, None, ALU.not_equal).then_inc(nonzero, 1)
            dve.wait_ge(flag_sum, 1)
            nc.vector.tensor_scalar(flag[:, :], s1_bank[0][0:1, 0:1], 0.0, None, ALU.is_gt).then_inc(flag_set, 1)
            dve.wait_ge(w_high, 4)
            nc.vector.scalar_tensor_tensor(wo[1][:, :, :], stage_wo, 1.0, wo[0][:, :, :].bitcast(F32), ALU.mult, ALU.subtract).then_inc(w_low, 1)
            dve.wait_ge(flag_set, 1)
            flagged = dve.value_load(flag[0:1, 0:1], min_val=0, max_val=1)

            def steps(general):
                for t in STEPS_BEFORE[1:]:
                    step(t, t % 2, general)
                with dve.Fori(LOOP_START, LOOP_END, 2) as t:
                    step(t, 0, general)
                    step(t + 1, 1, general)
                for t in STEPS_AFTER:
                    step(t, t % 2, general)

            with dve.If(flagged != 0):
                steps(True)
            with dve.Else():
                steps(False)


_INS = ["x", "ctx_2048", "mask_Bx1xSxS2_ff0", "L0_xattn_Wq", "L0_xattn_bq", "L0_xattn_Wk", "L0_xattn_bk", "L0_xattn_Wv",
        "L0_xattn_bv", "L0_xattn_Wo", "L0_xattn_bo", "L0_xattn_gamma", "L0_xattn_beta"]


def lay_out(name, a):
    if name[-2:] in ("Wq", "bq", "Wk", "bk"):
        lead, n = a.shape[:-1], a.shape[-1]
        return a.reshape(*lead, n // P, P // HD, HD).swapaxes(-1, -2).reshape(*lead, n)
    return a


def kernel(**inputs):
    import numpy as np
    import concourse.bacc as bacc
    from concourse.bass_utils import run_bass_kernel_spmd

    nc = bacc.Bacc("TRN2", target_bir_lowering=False, num_devices=1)
    arrays, args = {}, []
    for name in _INS:
        a = np.ascontiguousarray(lay_out(name, inputs[name]))
        arrays[f"in_{name}"] = a
        args.append(nc.dram_tensor(f"in_{name}", a.shape, mybir.dt.from_np(a.dtype), kind="ExternalInput").ap())
    out = nc.dram_tensor("out_y", inputs["x"].shape, F32, kind="ExternalOutput").ap()
    build(nc, *args, out)
    r = run_bass_kernel_spmd(nc, [arrays], core_ids=[0])
    return r.results[0]["out_y"]
```

```python
from contextlib import ExitStack

import concourse.bass as bass
from concourse import mybir

F32 = mybir.dt.float32
F32R = mybir.dt.float32r
BF16 = mybir.dt.bfloat16
I32 = mybir.dt.int32
ALU = mybir.AluOpType
ACT = mybir.ActivationFunctionType
AX = mybir.AxisListType

P = 128
HD = 16
KVH = 8
GROUPS = 4
NH = KVH * GROUPS
EPS = 1e-6
SCALE = 0.25
PAIRS = [(0, 0), (1, 0), (2, 0), (0, 1), (1, 1), (0, 2)]
PARTS = 3
Q_FIRST, Q_SIZES = (0, 2, 3), (2, 1, 1)
STACK = HD * len(PAIRS)
MROWS = STACK + PARTS

SLOTS = 32
TILES = NH
QUADS = 8
GRPS = 4
TURNS = ("c0", "c1", "x0", "x1")
PV_LAG = 5

MAX_COUNTS = (2, 1, 0, 2, 1, 1, 1, 2, 1, 1, 1, 1, 1, 1, 2, 1, 2, 1, 1, 1, 0, 2, 1, 1, 0, 2, 1, 1, 0, 0, 0, 0)
ATTEND_COUNTS = (0, 0, 0, 0, 0, 0, 0, 2, 1, 1, 2, 0, 1, 1, 2, 2, 1, 2, 1, 1, 1, 2, 1, 1, 2, 1, 1, 1, 2, 1, 1, 1)
FIRST_MAX_COUNTS = (0, 0, 0, 0, 0, 1, 1, 1, 1, 1, 1, 1, 2, 1, 1, 1, 0, 1, 1, 2, 2, 2, 2, 2, 2, 2, 2, 2, 0, 0, 0, 0)
PE_SIDE = {0: ["last_quad", "c0"], 1: ["c1"], 3: ["x0"], 5: ["x1", "k.0"], 6: ["k.1"], 7: ["v.0", "v.1"],
           8: ["vturn"], 9: ["q0.0"], 11: ["q0.1", "q1.0"], 12: ["q1.1"], 13: ["y0.0", "y0.1"], 15: ["y0.2"],
           16: ["y0.3"], 18: ["y1.0"], 19: ["y1.1"], 21: ["y1.2", "y1.3"], 24: ["q2.0"], 25: ["q2.1"],
           27: ["q3.0"], 28: ["q3.1"], 30: ["mturn"]}
LAST_PE_SIDE = ["last_quad", "y0.0", "y0.1", "y0.2", "y1.0", "y1.1", "y1.2", "y0.3", "y1.3"]
ACT_SIDE = {0: ["group2"], 1: ["c0", "c1"], 2: ["x0", "attn3"], 4: ["x1", "mid3"], 9: ["vturn", "kv"],
            12: ["mid0"], 13: ["group0"], 16: ["mid1"], 18: ["attn0"], 23: ["attn1"], 25: ["group1"],
            26: ["norm0"], 28: ["mid2"], 29: ["norm1"], 31: ["mturn", "attn2"]}
POOL_ORDER = ["c0", "c1", "x0", "rest3", "x1", "low3", "attn3", "rest0", "bias", "rest1", "low0", "low1", "attn0",
              "factors", "rest2", "attn1", "gamma0", "low2", "gamma1", "attn2"]
SUMS_FROM = {3: 5, 0: 31, 1: 41, 2: 54}
NORM_FROM = (37, 45)
SPLIT_FROM = 55


STACKED = 16 * 2 * PARTS


def max_tiles(t, s):
    counts = FIRST_MAX_COUNTS if isinstance(t, int) and t == -1 else MAX_COUNTS
    return range(sum(counts[:s]), sum(counts[:s + 1]))


def attend_tiles(s):
    return range(sum(ATTEND_COUNTS[:s]), sum(ATTEND_COUNTS[:s + 1]))


def due(eng, sem, count):
    if not isinstance(count, int) or count > 0:
        eng.wait_ge(sem, count)


def build(nc, x, ctx_in, mask, w_q, b_q, w_k, b_k, w_v, b_v, w_o, b_o, gamma, beta, out):
    NB, L, H = x.shape
    S = ctx_in.shape[1]
    LT, ST = L // P, S // P
    CH = H // P
    assert (LT, ST, CH, L, S) == (2, 2, 4, 256, 256) and NB % 2 == 0 and NB >= 6

    with ExitStack() as stack:
        def sb(name, shape, dt=F32):
            return stack.enter_context(nc.sbuf_tensor(name, shape, dt))

        def sem(name):
            return stack.enter_context(nc.semaphore(name))

        wq = [sb(f"wq_{n}", [P, CH, H], F32R) for n in "hl"]
        wo = [sb(f"wo_{n}", [P, CH, H], F32R) for n in "hl"]
        wk = [sb(f"wk_{n}", [P, CH, P], F32R) for n in "hl"]
        wv = [sb(f"wv_{n}", [P, CH, P], F32R) for n in "hl"]
        bias_q, bias_k, bias_v = sb("bias_q", [P, CH]), sb("bias_k", [P, 1]), sb("bias_v", [P, 1])
        gamma_row, beta_row, bo_row = sb("gamma_row", [P, H]), sb("beta_row", [P, H]), sb("bo_row", [P, H])
        ident, ident16 = sb("ident", [P, P]), sb("ident16", [P, P], BF16)
        ones = sb("ones", [P, 1])
        x_in, c_in = sb("x_in", [P, LT, H]), sb("c_in", [P, ST, H])
        turned = [[sb(f"{a}T_{n}", [P, CH, L], F32R) for n in "hl"] for a in "cx"]
        k_parts = sb("k_parts", [P, PARTS, S], BF16)
        k_rest = sb("k_rest", [P, S])
        q_parts = [sb(f"q_parts{g}", [P, n, PARTS, L], BF16) for g, n in enumerate(Q_SIZES)]
        q_rest = sb("q_rest", [P, CH, L])
        turned_full = [sb(f"turned_full{u}", [P, 2, L]) for u in range(2)]
        v_rows = [sb(f"v_rows{u}", [P, S]) for u in range(2)]
        q_stack = [sb(f"q_stack{u}", [P, NH, L], BF16) for u in range(2)]
        k_stack = [sb(f"k_stack{u}", [P, KVH, S], BF16) for u in range(2)]
        v_ones = [sb(f"v_ones{u}", [P, ST, KVH, 2 * HD]) for u in range(2)]
        neg_max = sb("neg_max", [P, LT, NH])
        neg_max_rest = sb("neg_max_rest", [P, LT, NH])
        max_parts = sb("max_parts", [P, LT, PARTS, NH], BF16)
        max_rows = sb("max_rows", [PARTS * NH, L], BF16)
        probs = sb("probs", [P, 8, 512])
        sums_t = sb("sums_t", [P, 512])
        recip = sb("recip", [P, 16])
        attn_t = sb("attn_t", [P, 256])
        attn = [sb(f"attn{i}", [P, L]) for i in range(2)]
        attn_parts = [[sb(f"attn_{n}{u}", [P, GRPS, L], F32R) for n in "hl"] for u in range(2)]
        resid = sb("resid", [P, LT, H])
        normed = sb("normed", [P, LT, H])
        stats, mean_var = sb("stats", [P, LT, 6]), sb("mean_var", [P, LT, 2])
        rstd, shift, power = sb("rstd", [P, LT]), sb("shift", [P, LT]), sb("power", [P, LT])
        scan = sb("scan", [P, 4])
        flag = sb("flag", [1, 1], I32)
        mask_in = sb("mask_in", [P, LT, S])
        mask_t = [sb(f"mask_t{u}", [P, ST, L]) for u in range(2)]

        s1_bank = [stack.enter_context(nc.psum_tensor(f"s1_bank{i}", [P, 512], F32)) for i in range(2)]
        s2_bank = [stack.enter_context(nc.psum_tensor(f"s2_bank{i}", [P, 512], F32)) for i in range(2)]
        sum_bank = stack.enter_context(nc.psum_tensor("sum_bank", [P, 512], F32))
        bank = {n: stack.enter_context(nc.psum_tensor(f"bank_{n}", [P, 512], F32)) for n in "abc"}
        turn_bank = [bank[n] for n in "acac"]
        q_bank = {0: bank["a"], 1: bank["b"]}
        y_bank = {0: bank["c"], 1: bank["a"]}

        q_scratch = [nc.dram_tensor(f"q_scratch{g}", [n * PARTS, P, L], BF16) for g, n in enumerate(Q_SIZES)]
        k_scratch = nc.dram_tensor("k_scratch", [PARTS, P, S], BF16)

        w_in = [sem(f"w_in{i}") for i in range(5)]
        biases_in, rows_in = sem("biases_in"), sem("rows_in")
        mask_scan_in = sem("mask_scan_in")
        x_loaded, c_loaded, resid_loaded = sem("x_loaded"), sem("c_loaded"), sem("resid_loaded")
        mask_loaded = sem("mask_loaded")
        k_out = sem("k_out")
        q_out = [sem(f"q_out{g}") for g in range(3)]
        stacked = [sem(f"stacked{g}") for g in range(3)]
        max_in = sem("max_in")
        y_out = sem("y_out")
        sp_passed, pool_passed, dve_passed = sem("sp_passed"), sem("pool_passed"), sem("dve_passed")
        consts = sem("consts")
        w_high, w_low = sem("w_high"), sem("w_low")
        wo_high, wo_low = sem("wo_high"), sem("wo_low")
        bias_scaled = sem("bias_scaled")
        scanned, nonzero, flag_sum, flag_set = sem("scanned"), sem("nonzero"), sem("flag_sum"), sem("flag_set")
        turned_pe, proj_pe, vturn_pe = sem("turned_pe"), sem("proj_pe"), sem("vturn_pe")
        s1_ready, mturn_pe, s2_ready = sem("s1_ready"), sem("mturn_pe"), sem("s2_ready")
        pv_done, y_ready = sem("pv_done"), sem("y_ready")
        turned_high, proj_high, v_ready = sem("turned_high"), sem("proj_high"), sem("v_ready")
        parts_mid = sem("parts_mid")
        max_rows_ready, exp_done, normed_act = sem("max_rows_ready"), sem("exp_done"), sem("normed_act")
        attn_high = sem("attn_high")
        s1_used, max_split = sem("s1_used"), sem("max_split")
        sums_turned, recip_done, attn_scaled, attn_back = (sem(n) for n in ("sums_turned", "recip_done", "attn_scaled", "attn_back"))
        resid_added, norm_stats = sem("resid_added"), sem("norm_stats")
        s1_masked, s2_masked, mask_turned = sem("s1_masked"), sem("s2_masked"), sem("mask_turned")
        turned_low, rest_done, parts_done, attn_low = sem("turned_low"), sem("rest_done"), sem("parts_done"), sem("attn_low")
        norm_factors = sem("norm_factors")
        resid_biased, gamma_done, out_ready = sem("resid_biased"), sem("gamma_done"), sem("out_ready")

        block = stack.enter_context(nc.Block())

        STEPS_BEFORE = range(-2, 2)
        LOOP_START, LOOP_END = 2, NB - 3
        STEPS_AFTER = range(NB - 2, NB + 1)

        def stages(t):
            if not isinstance(t, int):
                return True, True, True, True
            return 0 <= t + 2 < NB, 0 <= t + 1 < NB, 0 <= t < NB, 0 <= t - 1 < NB

        stage_wq = probs[:, 0:CH, :]
        stage_wo = probs[:, CH:2 * CH, :]
        stage_wk = resid[:, 0, :].rearrange("p (c n) -> p c n", c=CH)
        stage_wv = resid[:, 1, :].rearrange("p (c n) -> p c n", c=CH)
        scan_cols = NB * L * S // P // 2
        scan_part = [q_stack[i][:, :, :].rearrange("p h l -> p (h l)").bitcast(F32)[:, 0:scan_cols] for i in range(2)]

        @block.sync
        def _(sp):
            def rows(ap):
                return ap.rearrange("(t p) d -> p t d", p=P)

            def parts_out(b, g):
                sp.wait_ge(parts_done, 4 * b + g + 2)
                sp.sem_inc(sp_passed)
                due(sp, stacked[g], STACKED * b)
                sp.dma_start(q_scratch[g].rearrange("m p l -> p m l"),
                             q_parts[g][:, :, :, :].rearrange("p m a l -> p (m a) l")).then_inc(q_out[g], 16)

            def stack_group(b_parity, g):
                n, first = Q_SIZES[g], Q_FIRST[g]
                for kp in range(PARTS):
                    js = [j for j, pair in enumerate(PAIRS) if pair[1] == kp]
                    rows_of_pairs = slice(HD * js[0], HD * (js[-1] + 1))
                    sp.dma_start(q_stack[b_parity][rows_of_pairs, 8 * first:8 * (first + n), :].rearrange("r (m h) l -> r m (h l)", m=n),
                                 q_scratch[g].rearrange("(m a) (d h) l -> (a d) m (h l)", m=n, d=HD)[0:HD * len(js)]).then_inc(stacked[g], 16)
                    sp.dma_start(k_stack[b_parity][rows_of_pairs, 2 * first:2 * (first + n), :],
                                 k_scratch[kp].rearrange("(d h) l -> d h l", d=HD)[:, 2 * first:2 * (first + n), :]
                                 .unsqueeze(0).broadcast_to([len(js), HD, 2 * n, S])).then_inc(stacked[g], 16)

            def step(t, par, general):
                project, maxima, attend, output = stages(t)
                load = not isinstance(t, int) or t + 3 < NB
                if maxima:
                    due(sp, s2_ready, TILES * t)
                    sp.sem_inc(sp_passed)
                    sp.wait_ge(q_out[1], 16 * (t + 2))
                    stack_group(1 - par, 1)
                if maxima and general is not None:
                    with sp.If(general != 0):
                        due(sp, mask_turned, t + 1)
                        sp.dma_start(mask_in[:, :, :], rows(mask[t + 1, 0])).then_inc(mask_loaded, 16)
                if load:
                    sp.wait_ge(turned_pe, 4 * (t + 2) + 2)
                    sp.dma_start(c_in[:, :, :], rows(ctx_in[t + 3])).then_inc(c_loaded, 16)
                    sp.wait_ge(turned_pe, 4 * (t + 2) + 4)
                    sp.dma_start(x_in[:, :, :], rows(x[t + 3])).then_inc(x_loaded, 16)
                if maxima:
                    parts_out(t + 1, 2)
                if project:
                    b2 = t + 2
                    sp.wait_ge(parts_done, 4 * b2 + 1)
                    for g in range(3):
                        sp.sem_inc(sp_passed)
                        if g < 2:
                            due(sp, stacked[g], STACKED * b2)
                if maxima:
                    sp.wait_ge(q_out[2], 16 * (t + 2))
                    stack_group(1 - par, 2)
                if project:
                    due(sp, stacked[2], STACKED * b2)
                    sp.dma_start(k_scratch.rearrange("m p l -> p m l"), k_parts[:, :, :]).then_inc(k_out, 16)
                    parts_out(b2, 0)
                    sp.wait_ge(k_out, 16 * (b2 + 1))
                    sp.sem_inc(sp_passed)
                    sp.wait_ge(q_out[0], 16 * (b2 + 1))
                    sp.sem_inc(sp_passed)
                    due(sp, s2_ready, TILES * t + TILES // 2)
                    if isinstance(t, int) and t < 0:
                        sp.wait_ge(scanned, t + 3)
                    stack_group(par, 0)
                    parts_out(b2, 1)
                if maxima:
                    sp.wait_ge(max_rows_ready, t + 2)
                    sp.dma_start(q_stack[1 - par][STACK:MROWS, :, :], max_rows[:, :]).then_inc(max_in, 16)
                if attend:
                    if isinstance(t, int):
                        sp.wait_ge(w_low, 2)
                    due(sp, normed_act, 2 * t)
                    sp.dma_start(resid[:, :, :], rows(x[t])).then_inc(resid_loaded, 16)
                if output and isinstance(t, int) and t == NB:
                    for lt in range(LT):
                        sp.wait_ge(out_ready, 2 * (t - 1) + lt + 1)
                        sp.dma_start(out[t - 1, lt * P:(lt + 1) * P, :], normed[:, lt, :]).then_inc(y_out, 16)
                elif output:
                    sp.wait_ge(out_ready, 2 * t)
                    sp.dma_start(rows(out[t - 1]), normed[:, :, :]).then_inc(y_out, 16)

            sp.dma_start(c_in[:, :, :], rows(ctx_in[0])).then_inc(c_loaded, 16)
            sp.dma_start(stage_wk, w_k.rearrange("(c p) n -> p c n", p=P)).then_inc(w_in[0], 16)
            sp.dma_start(stage_wv, w_v.rearrange("(c p) n -> p c n", p=P)).then_inc(w_in[1], 16)
            sp.dma_start(x_in[:, :, :], rows(x[0])).then_inc(x_loaded, 16)
            for half in range(2):
                cols = slice(half * H // 2, (half + 1) * H // 2)
                sp.dma_start(stage_wq[:, :, cols], w_q.rearrange("(c p) n -> p c n", p=P)[:, :, cols]).then_inc(w_in[2 + half], 16)
            with nc.allow_non_contiguous_dma("biases, once"):
                sp.dma_start(bias_q[:, :], b_q.rearrange("(m p) -> p m", p=P)).then_inc(biases_in, 16)
                sp.dma_start(bias_k[:, :], b_k.rearrange("(p o) -> p o", o=1)).then_inc(biases_in, 16)
                sp.dma_start(bias_v[:, :], b_v.rearrange("(p o) -> p o", o=1)).then_inc(biases_in, 16)
            whole = mask.rearrange("b o l s -> (b o l s)").rearrange("(i p n) -> i p n", i=2, p=P)
            for i in range(2):
                sp.dma_start(scan_part[i], whole[i]).then_inc(mask_scan_in, 16)

            step(-2, 0, None)
            sp.dma_start(stage_wo, w_o.rearrange("(c p) n -> p c n", p=P)).then_inc(w_in[4], 16)
            for row, src in ((gamma_row, gamma), (beta_row, beta), (bo_row, b_o)):
                sp.dma_start(row[:, :], src.partition_broadcast(P)).then_inc(rows_in, 16)
            sp.wait_ge(flag_set, 1)
            general = sp.value_load(flag[0:1, 0:1], min_val=0, max_val=1)
            for t in STEPS_BEFORE[1:]:
                step(t, t % 2, general)
            with sp.Fori(LOOP_START, LOOP_END - 2, 2) as t:
                step(t, 0, general)
                step(t + 1, 1, general)
            for t in range(NB - 4, NB + 1):
                step(t, t % 2, general)
            sp.wait_ge(y_out, 16 * (NB + 1))

        @block.gpsimd
        def _(pool):
            for i, m in enumerate((ident, ident16)):
                nc.gpsimd.memset(m[:, :], 0.0).then_inc(consts, 1)
                pool.wait_ge(consts, 2 * i + 1)
                nc.gpsimd.affine_select(out=m[:, :], in_=m[:, :], compare_op=ALU.not_equal, fill=1.0, base=0,
                                        pattern=[[-1, P]], channel_multiplier=1).then_inc(consts, 1)
            nc.gpsimd.memset(ones[:, :], 1.0).then_inc(consts, 1)
            nc.gpsimd.memset(power[:, :], -0.5).then_inc(consts, 1)
            for u in range(2):
                nc.gpsimd.memset(v_ones[u][:, :, :, HD:2 * HD], 1.0).then_inc(consts, 1)
            for u in range(2):
                pool.wait_ge(consts, 8 + u)
                nc.gpsimd.memset(k_stack[u][STACK:MROWS, :, :], 1.0).then_inc(consts, 1)
            pool.wait_ge(consts, 10)

            def turned_rest(t, i):
                pool.wait_ge(turned_high, 4 * (t + 2) + i + 1)
                cols = slice(2 * (i % 2), 2 * (i % 2) + 2)
                high, low = turned[i // 2]
                nc.gpsimd.tensor_tensor(low[:, cols, :], turned_full[i % 2][:, :, :], high[:, cols, :].bitcast(F32),
                                        ALU.subtract).then_inc(turned_low, 1)

            def full_and_parts(n):
                if n == 0:
                    return k_rest[:, :], [k_parts[:, a, :] for a in range(PARTS)]
                first, size = Q_FIRST[n - 1], Q_SIZES[n - 1]
                return q_rest[:, first:first + size, :], [q_parts[n - 1][:, :, a, :] for a in range(PARTS)]

            def parts_rest(b, n):
                rest, part = full_and_parts(n)
                pool.wait_ge(proj_high, 4 * b + n + 1)
                nc.gpsimd.tensor_tensor(rest, rest, part[0], ALU.subtract).then_inc(rest_done, 1)

            def parts_lowest(b, n):
                rest, part = full_and_parts(n)
                pool.wait_ge(parts_mid, 4 * b + n + 1)
                nc.gpsimd.tensor_tensor(part[2], rest, part[1], ALU.subtract).then_inc(parts_done, 1)

            def split_attn(b, par, grp):
                pool.wait_ge(attn_high, 4 * b + grp + 1)
                high, low = (attn_parts[par][i][:, grp, :] for i in range(2))
                nc.gpsimd.tensor_tensor(low, attn[grp % 2][:, :], high.bitcast(F32), ALU.subtract).then_inc(attn_low, 1)

            def norm_scale(b, tiles=slice(0, LT), done=0):
                pool.wait_ge(norm_stats, 4 * b + 2 * tiles.stop)
                pool.sem_inc(pool_passed)
                nc.gpsimd.tensor_scalar(rstd[:, tiles], mean_var[:, tiles, 1], EPS, None, ALU.add).then_inc(norm_factors, 1)
                pool.wait_ge(norm_factors, 4 * b + done + 1)
                nc.gpsimd.tensor_tensor(rstd[:, tiles], rstd[:, tiles], power[:, tiles], ALU.pow).then_inc(norm_factors, 1)
                pool.wait_ge(norm_factors, 4 * b + done + 2)
                nc.gpsimd.tensor_tensor(shift[:, tiles], mean_var[:, tiles, 0], rstd[:, tiles], ALU.mult).then_inc(norm_factors, 1)
                pool.wait_ge(norm_factors, 4 * b + done + 3)
                pool.sem_inc(pool_passed)
                nc.gpsimd.tensor_scalar(shift[:, tiles], shift[:, tiles], -1.0, None, ALU.mult).then_inc(norm_factors, 1)

            def gamma_beta(b, lt):
                pool.wait_ge(normed_act, 2 * b + lt + 1)
                nc.gpsimd.tensor_tensor(normed[:, lt, :], normed[:, lt, :], gamma_row[:, :], ALU.mult).then_inc(gamma_done, 1)
                pool.wait_ge(gamma_done, 2 * b + lt + 1)
                nc.gpsimd.tensor_tensor(normed[:, lt, :], normed[:, lt, :], beta_row[:, :], ALU.add).then_inc(out_ready, 1)

            def add_bias(b):
                pool.wait_ge(rows_in, 48)
                pool.wait_ge(resid_loaded, 16 * (b + 1))
                nc.gpsimd.tensor_tensor(resid[:, :, :], resid[:, :, :], bo_row[:, :].unsqueeze(1).broadcast_to([P, LT, H]),
                                        ALU.add).then_inc(resid_biased, 1)

            def step(t, par):
                project, maxima, attend, output = stages(t)
                for what in POOL_ORDER:
                    if what == "bias" and isinstance(t, int) and t == -1:
                        pool.wait_ge(wo_high, 1)
                        nc.gpsimd.tensor_tensor(wo[1][:, :, :], stage_wo, wo[0][:, :, :].bitcast(F32), ALU.subtract).then_inc(wo_low, 1)
                    if what in TURNS and project:
                        turned_rest(t, TURNS.index(what))
                    if what in ("rest0", "rest1", "rest2") and project:
                        parts_rest(t + 2, int(what[4]))
                    if what in ("low0", "low1", "low2") and project:
                        parts_lowest(t + 2, int(what[3]))
                    if what == "rest3" and maxima:
                        parts_rest(t + 1, 3)
                    if what == "low3" and maxima:
                        parts_lowest(t + 1, 3)
                    if what == "attn3" and output:
                        split_attn(t - 1, 1 - par, 3)
                    if what in ("attn0", "attn1", "attn2") and attend:
                        split_attn(t, par, int(what[4]))
                    last_step = isinstance(t, int) and t == NB
                    if what == "bias" and output and not last_step:
                        add_bias(t - 1)
                    if what == "factors" and last_step:
                        for lt in range(LT):
                            norm_scale(t - 1, slice(lt, lt + 1), 4 * lt)
                    if what == "factors" and output and not last_step:
                        norm_scale(t - 1)
                    if what in ("gamma0", "gamma1") and output and not last_step:
                        gamma_beta(t - 1, int(what[5]))

            for t in STEPS_BEFORE:
                step(t, t % 2)
            with pool.Fori(LOOP_START, LOOP_END, 2) as t:
                step(t, 0)
                step(t + 1, 1)
            for t in STEPS_AFTER:
                step(t, t % 2)

        @block.tensor
        def _(pe):
            def turn(t, i):
                b2, src = t + 2, (c_in, x_in)[i // 2]
                if i == 0:
                    pe.wait_ge(c_loaded, 16 * (b2 + 1))
                    due(pe, resid_added, 2 * (t - 1))
                    due(pe, proj_high, 4 * (b2 - 1) + 2)
                if i == 1:
                    due(pe, max_rows_ready, t + 1)
                if i == 2:
                    pe.wait_ge(x_loaded, 16 * (b2 + 1))
                if i >= 2:
                    pe.wait_ge(turned_high, 4 * b2 + i - 1)
                for c in range(2):
                    for lt in range(LT):
                        f = 2 * (i % 2) + c
                        last = nc.tensor.transpose(turn_bank[i][:, c * L + lt * P:c * L + (lt + 1) * P],
                                                   src[:, lt, f * P:(f + 1) * P], ident[:, :])
                last.then_inc(turned_pe, 1)

            def project_half(dst, w, cols, src, half, inc=None):
                for c in range(half * CH // 2, (half + 1) * CH // 2):
                    for a, b in ((0, 0), (0, 1), (1, 0)):
                        last = nc.tensor.matmul(dst, w[a][:, c, cols], src[b][:, c, :],
                                                start=(c == 0 and (a, b) == (0, 0)), stop=(c == CH - 1 and a == 1))
                if inc is not None and half == 1:
                    last.then_inc(inc, 1)

            def y_chunk(b, par, lt, c):
                for m, n in ((0, 0), (0, 1), (1, 0)):
                    last = nc.tensor.matmul(y_bank[lt][:, :], attn_parts[par][m][:, c, lt * P:(lt + 1) * P], wo[n][:, c, :],
                                            start=(c == 0 and (m, n) == (0, 0)), stop=(c == CH - 1 and m == 1))
                if c == CH - 1:
                    last.then_inc(y_ready, 1)

            def sum_findings():
                pe.wait_ge(nonzero, 1)
                nc.tensor.matmul(s1_bank[0][0:1, 0:1], scan[:, 3:4], ones[:, :], start=True, stop=True).then_inc(flag_sum, 1)
                pe.wait_ge(flag_set, 1)

            def scores_for_max(b, par, head):
                if head in (8 * m for m in Q_FIRST):
                    pe.wait_ge(stacked[Q_FIRST.index(head // 8)], STACKED * (b + 1))
                if not isinstance(b, int) or b > 0 or head >= 2:
                    pe.wait_ge(s1_used, NH * b + head - 1)
                for lt in range(LT):
                    last = nc.tensor.matmul(s1_bank[head % 2][:, lt * S:(lt + 1) * S],
                                            q_stack[par][0:STACK, head, lt * P:(lt + 1) * P],
                                            k_stack[par][0:STACK, head // GROUPS, :], start=True, stop=True)
                last.then_inc(s1_ready, 1)

            def scores(b, par, j):
                grp, st, kv, pair = j // 8, j // 4 % 2, j // 2 % 2, j % 2
                kvh = 2 * grp + kv
                head = kvh * GROUPS + 2 * pair
                if j == 0:
                    pe.wait_ge(max_in, 16 * (b + 1))
                if not isinstance(b, int) or b > 0 or j >= 2:
                    pe.wait_ge(exp_done, TILES * b + j - 1)
                nc.tensor.matmul(s2_bank[j % 2][:, :], k_stack[par][0:MROWS, kvh, st * P:(st + 1) * P],
                                 q_stack[par][0:MROWS, head:head + 2, :], start=True, stop=True).then_inc(s2_ready, 1)

            def weighted_sums(b, par, q):
                grp, st = q // 2, q % 2
                pe.wait_ge(exp_done, TILES * b + 4 * q + 4)
                if q == 0:
                    pe.wait_ge(v_ready, b + 1)
                if st == 0:
                    due(pe, sums_turned, 4 * b + grp)
                for c in range(4):
                    last = nc.tensor.matmul(sum_bank[32 * c:32 * (c + 1), :], v_ones[par][:, st, 2 * grp + c // 2, :],
                                            probs[:, 4 * (q % 2) + c, :], start=(st == 0), stop=(st == 1))
                last.then_inc(pv_done, 1)

            def side(t, par, what):
                project, maxima, attend, output = stages(t)
                b2 = t + 2
                what, part = what.split(".") if "." in what else (what, "0")
                part = int(part)
                if what in TURNS and project:
                    turn(t, TURNS.index(what))
                if what == "k" and project:
                    if part == 0:
                        pe.wait_ge(turned_low, 4 * b2 + 2)
                        due(pe, proj_high, 4 * b2)
                        if isinstance(t, int) and t == -2:
                            pe.wait_ge(w_low, 1)
                    project_half(bank["b"][:, 0:S], wk, slice(0, P), turned[0], part)
                if what == "v" and project:
                    if part == 0 and isinstance(t, int) and t == -2:
                        pe.wait_ge(w_low, 2)
                    project_half(bank["b"][:, S:2 * S], wv, slice(0, P), turned[0], part, proj_pe)
                if what == "last_quad" and output:
                    weighted_sums(t - 1, 1 - par, QUADS - 1)
                if what == "vturn" and maxima:
                    if project:
                        pe.wait_ge(turned_high, 4 * b2 + 4)
                    else:
                        pe.wait_ge(max_rows_ready, t + 1)
                    pe.wait_ge(proj_high, 4 * (t + 1) + 1)
                    for st in range(ST):
                        last = nc.tensor.transpose(bank["c"][:, st * P:(st + 1) * P],
                                                   v_rows[1 - par][:, st * P:(st + 1) * P], ident[:, :])
                    last.then_inc(vturn_pe, 1)
                if what[0] == "q" and project:
                    m, b = int(what[1]), t + 2
                    if part == 0 and m == 0:
                        pe.wait_ge(turned_low, 4 * b + 4)
                        if isinstance(t, int) and t == -2:
                            pe.wait_ge(w_low, 3)
                    if part == 0 and m == 2 and isinstance(t, int) and t == -2:
                        pe.wait_ge(w_low, 4)
                    if part == 0 and m == 3:
                        pe.wait_ge(proj_high, 4 * b + 3)
                    if part == 0 and m == 2:
                        pe.wait_ge(proj_high, 4 * b + 1)
                    project_half(q_bank[m // 2][:, m % 2 * L:(m % 2 + 1) * L], wq, slice(m * P, (m + 1) * P), turned[1],
                                 part, proj_pe if m > 0 else None)
                if what[0] == "y" and output:
                    lt = int(what[1])
                    if lt == 0:
                        pe.wait_ge(attn_low, 4 * (t - 1) + part + 1)
                    if part == 0 and lt == 0:
                        if isinstance(t, int):
                            pe.wait_ge(wo_low, 1)
                        if maxima:
                            pe.wait_ge(v_ready, t + 2)
                        else:
                            pe.wait_ge(resid_added, 2 * (t - 1))
                            pe.wait_ge(max_rows_ready, NB)
                    if part == 0 and lt == 1:
                        if project:
                            pe.wait_ge(proj_high, 4 * b2 + 2)
                        else:
                            pe.wait_ge(resid_added, 2 * (t - 1))
                    y_chunk(t - 1, 1 - par, lt, part)
                if what == "mturn" and maxima:
                    if output:
                        pe.wait_ge(resid_added, 2 * (t - 1) + 1)
                    else:
                        pe.wait_ge(v_ready, t + 2)
                    pe.wait_ge(max_split, 4 * (t + 2))
                    rows = bank["c"][:, :].bitcast(BF16)
                    for lt in range(LT):
                        last = nc.tensor.transpose(rows[0:PARTS * NH, lt * P:(lt + 1) * P],
                                                   max_parts[:, lt, :, :].rearrange("p a h -> p (a h)"), ident16[:, :])
                    last.then_inc(mturn_pe, 1)

            def step(t, par):
                project, maxima, attend, output = stages(t)
                for s in range(SLOTS):
                    attend_now = attend_tiles(s) if attend else []
                    max_now = max_tiles(t, s) if maxima else []
                    for i in range(2):
                        for j in attend_now[i:i + 1]:
                            scores(t, par, j)
                            if j >= PV_LAG and (j - PV_LAG) % 4 == 0:
                                weighted_sums(t, par, (j - PV_LAG) // 4)
                        for head in max_now[i:i + 1]:
                            if isinstance(t, int) and t == -1 and head == 0:
                                sum_findings()
                            scores_for_max(t + 1, 1 - par, head)
                    last_step = isinstance(t, int) and t == NB
                    for what in (LAST_PE_SIDE if last_step and s == 0 else PE_SIDE.get(s, []) if not last_step else []):
                        side(t, par, what)

            pe.wait_ge(consts, 10)
            step(-2, 0)
            for t in STEPS_BEFORE[1:]:
                step(t, t % 2)
            with pe.Fori(LOOP_START, LOOP_END, 2) as t:
                step(t, 0)
                step(t + 1, 1)
            for t in STEPS_AFTER:
                step(t, t % 2)

        @block.scalar
        def _(act):
            def turned_out(t, i):
                act.wait_ge(turned_pe, 4 * (t + 2) + i + 1)
                if i == 0:
                    due(act, proj_pe, 4 * (t + 1) + 1)
                if i == 2:
                    due(act, proj_pe, 4 * (t + 2))
                due(act, turned_low, 4 * (t + 2) + i - 1)
                src = turn_bank[i][:, :].rearrange("p (c l) -> p c l", c=2)
                nc.scalar.activation(turned[i // 2][0][:, 2 * (i % 2):2 * (i % 2) + 2, :], src, ACT.Copy)
                nc.scalar.activation(turned_full[i % 2][:, :, :], src, ACT.Copy).then_inc(turned_high, 1)

            def exp_tile(t, j, general):
                act.wait_ge(s2_masked if general else s2_ready, TILES * t + j + 1)
                if j % 4 == 0:
                    due(act, pv_done, QUADS * t + j // 4 - 1)
                nc.scalar.activation(probs[:, j % 8, :], s2_bank[j % 2][:, :], ACT.Exp).then_inc(exp_done, 1)

            def q_group_out(b, g):
                act.wait_ge(proj_pe, 4 * b + 2 + g)
                due(act, q_out[g], 16 * b)
                for i in range(Q_SIZES[g]):
                    m = Q_FIRST[g] + i
                    src, bias = q_bank[m // 2][:, m % 2 * L:(m % 2 + 1) * L], bias_q[:, m:m + 1]
                    nc.scalar.activation(q_parts[g][:, i, 0, :], src, ACT.Identity, bias=bias)
                    last = nc.scalar.activation(q_rest[:, m, :], src, ACT.Identity, bias=bias)
                last.then_inc(proj_high, 1)

            def middle(b, n):
                act.wait_ge(rest_done, 4 * b + n + 1)
                if n == 0:
                    dst, rest = k_parts[:, 1, :], k_rest[:, :]
                else:
                    first, size = Q_FIRST[n - 1], Q_SIZES[n - 1]
                    dst, rest = q_parts[n - 1][:, :, 1, :], q_rest[:, first:first + size, :]
                nc.scalar.activation(dst, rest, ACT.Copy).then_inc(parts_mid, 1)

            def attn_out(b, par, grp):
                act.wait_ge(attn_back, 4 * b + grp + 1)
                if grp == 0:
                    due(act, y_ready, 2 * (b - 1))
                nc.scalar.activation(attn_parts[par][0][:, grp, :], attn[grp % 2][:, :], ACT.Copy).then_inc(attn_high, 1)

            def side(t, par, what):
                project, maxima, attend, output = stages(t)
                if what in TURNS and project:
                    turned_out(t, TURNS.index(what))
                if what == "kv" and project:
                    b2 = t + 2
                    act.wait_ge(proj_pe, 4 * b2 + 1)
                    due(act, k_out, 16 * b2)
                    nc.scalar.activation(k_parts[:, 0, :], bank["b"][:, 0:S], ACT.Identity, bias=bias_k[:, 0:1])
                    nc.scalar.activation(k_rest[:, :], bank["b"][:, 0:S], ACT.Identity, bias=bias_k[:, 0:1])
                    due(act, vturn_pe, b2 - 1)
                    nc.scalar.activation(v_rows[par][:, :], bank["b"][:, S:2 * S], ACT.Identity,
                                         bias=bias_v[:, 0:1]).then_inc(proj_high, 1)
                if what == "vturn" and maxima:
                    act.wait_ge(vturn_pe, t + 2)
                    due(act, pv_done, QUADS * t)
                    nc.scalar.activation(v_ones[1 - par][:, :, :, 0:HD],
                                         bank["c"][:, 0:S].rearrange("p (s k d) -> p s k d", s=ST, k=KVH),
                                         ACT.Copy).then_inc(v_ready, 1)
                if what in ("group0", "group1") and project:
                    q_group_out(t + 2, int(what[5]))
                if what == "group2" and maxima:
                    q_group_out(t + 1, 2)
                if what in ("mid0", "mid1", "mid2") and project:
                    middle(t + 2, int(what[3]))
                if what == "mid3" and maxima:
                    middle(t + 1, 3)
                if what in ("attn0", "attn1", "attn2") and attend:
                    attn_out(t, par, int(what[4]))
                if what == "attn3" and output:
                    attn_out(t - 1, 1 - par, 3)
                if what in ("norm0", "norm1") and output:
                    lt = int(what[4])
                    act.wait_ge(norm_factors, 4 * t + (4 * lt if isinstance(t, int) and t == NB else 0))
                    if lt == 0:
                        due(act, y_out, 16 * (t - 1))
                    nc.scalar.activation(normed[:, lt, :], resid[:, lt, :], ACT.Identity, bias=shift[:, lt:lt + 1],
                                         scale=rstd[:, lt:lt + 1]).then_inc(normed_act, 1)
                if what == "mturn" and maxima:
                    act.wait_ge(mturn_pe, t + 2)
                    due(act, max_in, 16 * (t + 1))
                    nc.scalar.activation(max_rows[:, :], bank["c"][:, :].bitcast(BF16)[0:PARTS * NH, 0:L],
                                         ACT.Copy).then_inc(max_rows_ready, 1)

            def weight_high(i, staged, w, scale=1.0, cols=slice(None)):
                act.wait_ge(w_in[i], 16)
                nc.scalar.activation(w[0][:, :, cols], staged[:, :, cols], ACT.Copy, scale=scale).then_inc(w_high, 1)

            def step(t, par, general):
                attend = stages(t)[2]
                for s in range(SLOTS):
                    if isinstance(t, int) and t == -2:
                        if "x0" in ACT_SIDE.get(s, []):
                            weight_high(0, stage_wk, wk)
                            weight_high(1, stage_wv, wv)
                        if "kv" in ACT_SIDE.get(s, []):
                            for half in range(2):
                                weight_high(2 + half, stage_wq, wq, SCALE, slice(half * H // 2, (half + 1) * H // 2))
                            act.wait_ge(biases_in, 48)
                            nc.scalar.activation(bias_q[:, :], bias_q[:, :], ACT.Copy, scale=SCALE).then_inc(bias_scaled, 1)
                            act.wait_ge(bias_scaled, 1)
                    for j in attend_tiles(s) if attend else []:
                        exp_tile(t, j, general)
                    for what in ACT_SIDE.get(s, []):
                        side(t, par, what)
                        if what == "kv" and isinstance(t, int) and t == -1:
                            act.wait_ge(w_in[4], 16)
                            nc.scalar.activation(wo[0][:, :, :], stage_wo, ACT.Copy).then_inc(wo_high, 1)

            step(-2, 0, False)
            step(-1, 1, False)
            act.wait_ge(w_low, 4)
            act.wait_ge(wo_low, 1)
            act.wait_ge(flag_set, 1)
            flagged = act.value_load(flag[0:1, 0:1], min_val=0, max_val=1)

            def steps(general):
                for t in STEPS_BEFORE[2:]:
                    step(t, t % 2, general)
                with act.Fori(LOOP_START, LOOP_END, 2) as t:
                    step(t, 0, general)
                    step(t + 1, 1, general)
                for t in STEPS_AFTER:
                    step(t, t % 2, general)

            with act.If(flagged != 0):
                steps(True)
            with act.Else():
                steps(False)

        @block.vector
        def _(dve):
            def take_max(b, par, head, general):
                tile = s1_bank[head % 2][:, :].rearrange("p (t s) -> p t s", t=LT)
                dve.wait_ge(s1_ready, NH * b + head + 1)
                if general:
                    if head == 0:
                        dve.wait_ge(mask_loaded, 16 * (b + 1))
                    nc.vector.tensor_tensor(tile, tile, mask_in[:, :, :], ALU.add).then_inc(s1_masked, 1)
                    dve.wait_ge(s1_masked, NH * b + head + 1)
                nc.vector.tensor_reduce(neg_max[:, :, head], tile, AX.X, ALU.max,
                                        negate=True).then_inc(s1_used, 1)

            def add_mask(b, par, j):
                st = j // 4 % 2
                tile = s2_bank[j % 2][:, :].rearrange("p (h l) -> p h l", h=2)
                if j == 0:
                    dve.wait_ge(mask_turned, b + 1)
                dve.wait_ge(s2_ready, TILES * b + j + 1)
                nc.vector.tensor_tensor(tile, tile, mask_t[par][:, st, :].unsqueeze(1).broadcast_to([P, 2, L]),
                                        ALU.add).then_inc(s2_masked, 1)

            def turn_mask(b, par):
                for i in range(L // 32):
                    lt, r = i // 4, 32 * (i % 4)
                    for q in range(4):
                        src = mask_in[r:r + 32, lt, :].rearrange("p (t q s) -> p t q s", t=ST, q=4)[:, :, q, :]
                        last = nc.vector.transpose(mask_t[par][32 * q:32 * (q + 1), :, 32 * i:32 * (i + 1)], src)
                last.then_inc(mask_turned, 1)

            def split_max(b, i):
                nm = neg_max[:, :, :]
                part = [max_parts[:, :, a, :] for a in range(PARTS)]
                if i == 0:
                    dve.wait_ge(s1_used, NH * (b + 1))
                    due(dve, mturn_pe, b)
                    op = nc.vector.tensor_copy(part[0], nm)
                else:
                    dve.wait_ge(max_split, 4 * b + i)
                if i == 1:
                    op = nc.vector.tensor_tensor(neg_max_rest[:, :, :], nm, part[0], ALU.subtract)
                if i == 2:
                    op = nc.vector.tensor_copy(part[1], neg_max_rest[:, :, :])
                if i == 3:
                    op = nc.vector.tensor_tensor(part[2], neg_max_rest[:, :, :], part[1], ALU.subtract)
                op.then_inc(max_split, 1)

            def finish_sums(b, grp, i):
                n = 4 * b + grp + 1
                if i == 0:
                    dve.wait_ge(pv_done, QUADS * b + 2 * grp + 2)
                    nc.vector.transpose(sums_t[:, :], sum_bank[:, :]).then_inc(sums_turned, 1)
                if i == 1:
                    dve.wait_ge(sums_turned, n)
                    nc.vector.reciprocal(recip[:, :], sums_t[:, :].rearrange("p (n r) -> p n r", r=32)[:, :, HD]).then_inc(recip_done, 1)
                if i == 2:
                    dve.wait_ge(recip_done, n)
                    nc.vector.tensor_tensor(attn_t[:, :].rearrange("p (n g d) -> p g n d", g=2, d=HD),
                                            sums_t[:, :].rearrange("p (g n r) -> p g n r", g=2, r=32)[:, :, :, 0:HD],
                                            recip[:, :].rearrange("p (g n) -> p g n", g=2).unsqueeze(3).broadcast_to([P, 2, 8, HD]),
                                            ALU.mult).then_inc(attn_scaled, 1)
                if i == 3:
                    dve.wait_ge(attn_scaled, n)
                    due(dve, attn_low, n - 2)
                    nc.vector.transpose(attn[grp % 2][:, :], attn_t[:, :]).then_inc(attn_back, 1)

            def norm(b, lt, i):
                n = 4 * b + 2 * lt
                if i == 0:
                    dve.wait_ge(y_ready, 2 * b + lt + 1)
                    if lt == 0:
                        dve.wait_ge(resid_biased, b + 1)
                    nc.vector.tensor_tensor(resid[:, lt, :], y_bank[lt][:, :], resid[:, lt, :], ALU.add).then_inc(resid_added, 1)
                if i == 1:
                    dve.wait_ge(resid_added, 2 * b + lt + 1)
                    nc.vector.bn_stats(stats[:, lt, :], resid[:, lt, :]).then_inc(norm_stats, 1)
                if i == 2:
                    dve.wait_ge(norm_stats, n + 1)
                    dve.sem_inc(dve_passed)
                    nc.vector.bn_aggr(mean_var[:, lt, :], stats[:, lt, :]).then_inc(norm_stats, 1)

            def step(t, par, general):
                project, maxima, attend, output = stages(t)
                for s in range(SLOTS):
                    attend_now = attend_tiles(s) if attend and general else []
                    max_now = max_tiles(t, s) if maxima else []
                    for k in range(2):
                        for j in attend_now[k:k + 1]:
                            add_mask(t, par, j)
                        for head in max_now[k:k + 1]:
                            take_max(t + 1, 1 - par, head, general)
                        i = 2 * s + k
                        for grp, start in SUMS_FROM.items():
                            if 0 <= i - start < 4:
                                if grp == 3 and output:
                                    finish_sums(t - 1, 3, i - start)
                                if grp < 3 and attend:
                                    finish_sums(t, grp, i - start)
                        if output:
                            for lt in range(LT):
                                if 0 <= i - NORM_FROM[lt] < 3:
                                    norm(t - 1, lt, i - NORM_FROM[lt])
                        if maxima and 0 <= i - SPLIT_FROM < 4:
                            split_max(t + 1, i - SPLIT_FROM)
                    if isinstance(t, int) and t == NB and 2 * s >= SUMS_FROM[3] + 4 > 2 * (s - 1):
                        dve.wait_ge(rows_in, 48)
                        dve.wait_ge(resid_loaded, 16 * t)
                        nc.vector.tensor_tensor(resid[:, :, :], resid[:, :, :], bo_row[:, :].unsqueeze(1).broadcast_to([P, LT, H]),
                                                ALU.add).then_inc(resid_biased, 1)
                if general and maxima:
                    turn_mask(t + 1, 1 - par)
                if isinstance(t, int) and t == NB:
                    dve.wait_ge(rows_in, 48)
                    for lt in range(LT):
                        n = 2 * (t - 1) + lt + 1
                        dve.wait_ge(normed_act, n)
                        nc.vector.tensor_tensor(normed[:, lt, :], normed[:, lt, :], gamma_row[:, :], ALU.mult).then_inc(gamma_done, 1)
                        dve.wait_ge(gamma_done, n)
                        nc.vector.tensor_tensor(normed[:, lt, :], normed[:, lt, :], beta_row[:, :], ALU.add).then_inc(out_ready, 1)

            def weight_low(i, staged, w, scale=1.0, cols=slice(None)):
                dve.wait_ge(w_high, i + 1)
                nc.vector.scalar_tensor_tensor(w[1][:, :, cols], staged[:, :, cols], scale, w[0][:, :, cols].bitcast(F32),
                                               ALU.mult, ALU.subtract).then_inc(w_low, 1)

            weight_low(0, stage_wk, wk)
            weight_low(1, stage_wv, wv)
            for half in range(2):
                weight_low(2 + half, stage_wq, wq, SCALE, slice(half * H // 2, (half + 1) * H // 2))
            dve.wait_ge(mask_scan_in, 32)
            for i in range(2):
                nc.vector.tensor_reduce(scan[:, i:i + 1], scan_part[i], AX.X, ALU.max, apply_absolute_value=True).then_inc(scanned, 1)
            dve.wait_ge(scanned, 2)
            nc.vector.tensor_tensor(scan[:, 2:3], scan[:, 0:1], scan[:, 1:2], ALU.max).then_inc(scanned, 1)
            dve.wait_ge(scanned, 3)
            nc.vector.tensor_scalar(scan[:, 3:4], scan[:, 2:3], 0.0, None, ALU.not_equal).then_inc(nonzero, 1)
            dve.wait_ge(flag_sum, 1)
            nc.vector.tensor_scalar(flag[:, :], s1_bank[0][0:1, 0:1], 0.0, None, ALU.is_gt).then_inc(flag_set, 1)
            dve.wait_ge(flag_set, 1)
            flagged = dve.value_load(flag[0:1, 0:1], min_val=0, max_val=1)

            def steps(general):
                for t in STEPS_BEFORE[1:]:
                    step(t, t % 2, general)
                with dve.Fori(LOOP_START, LOOP_END, 2) as t:
                    step(t, 0, general)
                    step(t + 1, 1, general)
                for t in STEPS_AFTER:
                    step(t, t % 2, general)

            with dve.If(flagged != 0):
                steps(True)
            with dve.Else():
                steps(False)


_INS = ["x", "ctx_2048", "mask_Bx1xSxS2_ff0", "L0_xattn_Wq", "L0_xattn_bq", "L0_xattn_Wk", "L0_xattn_bk", "L0_xattn_Wv",
        "L0_xattn_bv", "L0_xattn_Wo", "L0_xattn_bo", "L0_xattn_gamma", "L0_xattn_beta"]


def lay_out(name, a):
    if name[-2:] in ("Wq", "bq", "Wk", "bk"):
        lead, n = a.shape[:-1], a.shape[-1]
        return a.reshape(*lead, n // P, P // HD, HD).swapaxes(-1, -2).reshape(*lead, n)
    return a


def kernel(**inputs):
    import numpy as np
    import concourse.bacc as bacc
    from concourse.bass_utils import run_bass_kernel_spmd

    nc = bacc.Bacc("TRN2", target_bir_lowering=False, num_devices=1)
    arrays, args = {}, []
    for name in _INS:
        a = np.ascontiguousarray(lay_out(name, inputs[name]))
        arrays[f"in_{name}"] = a
        args.append(nc.dram_tensor(f"in_{name}", a.shape, mybir.dt.from_np(a.dtype), kind="ExternalInput").ap())
    out = nc.dram_tensor("out_y", inputs["x"].shape, F32, kind="ExternalOutput").ap()
    build(nc, *args, out)
    r = run_bass_kernel_spmd(nc, [arrays], core_ids=[0])
    return r.results[0]["out_y"]
```
